# Optimizing a Trainium2 kernel written in Bass

```python
import numpy as np
import jax
import jax.numpy as jnp

def _softmax(x, axis=-1):
    return jax.nn.softmax(x, axis=axis)

def _gelu(x):
    return jax.nn.gelu(x, approximate=True)

def _silu(x):
    return jax.nn.silu(x)

def _sigmoid(x):
    return jax.nn.sigmoid(x)

def _layernorm(x, axis=-1, eps=1e-05):
    m = jnp.mean(x, axis=axis, keepdims=True)
    v = jnp.var(x, axis=axis, keepdims=True)
    return (x - m) / jnp.sqrt(v + eps)

def _scatter_add(tgt, idx, src, axis=0):
    return tgt.at[idx].add(src)

def _segment_sum(src, seg, n):
    return jax.ops.segment_sum(src, seg, n)
kernel_name = 'mk_gnn_resnorm_d4_gnn_r8_cbe38e'

def setup_inputs(seed: int=0):
    np.random.seed(seed)
    _w = jnp.asarray

    def _rec_inputs():
        import jax
        import jax.numpy as jnp
        _gk = jax.random.key(seed)
        x = -0.000202 + 1 * jax.random.normal(jax.random.fold_in(_gk, 1), (6250, 128), jnp.float32)
        _s = jax.random.randint(jax.random.fold_in(_gk, 2), (100000,), 0, 6250, jnp.int32)
        _d = jax.random.randint(jax.random.fold_in(_gk, 3), (100000,), 0, 6250, jnp.int32)
        _loop = jnp.arange(6250, dtype=jnp.int32)
        src = jnp.concatenate([_s, _d, _loop])
        dst = jnp.concatenate([_d, _s, _loop])
        _o = jnp.argsort(dst, stable=True)
        src = src[_o]
        dst = dst[_o]
        edge_attr_2 = 0.000126197 + 0.999763 * jax.random.normal(jax.random.fold_in(_gk, 11), (206250, 2), jnp.float32)
        edge_type_50 = jax.random.randint(jax.random.fold_in(_gk, 13), (206250,), 0, 50, jnp.int32)
        return (x, src, dst, edge_attr_2, edge_type_50)
    x, src, dst, edge_attr_2, edge_type_50 = _rec_inputs()

    def _L0_gnn_setup():
        import jax, jax.numpy as jnp
        import numpy as np
        N_NODES = 6250
        IN_CH = 128
        OUT_CH = 128
        N_EDGES = 80000
        key = jax.random.key(seed)
        k1, k2, k3, k4 = jax.random.split(key, 4)
        x = jax.random.normal(k1, (N_NODES, IN_CH), dtype=jnp.float32)
        edge_index = jax.random.randint(k2, (2, N_EDGES), 0, N_NODES, dtype=jnp.int64)
        bound = 1.0 / np.sqrt(2 * IN_CH)
        W = jax.random.uniform(k3, (OUT_CH, 2 * IN_CH), minval=-bound, maxval=bound, dtype=jnp.float32)
        b = jax.random.uniform(k4, (OUT_CH,), minval=-bound, maxval=bound, dtype=jnp.float32)
        return {'x': x, 'edge_index': edge_index, 'W': W, 'b': b}
    _L0_gnn_all = _L0_gnn_setup()
    _L0_gnn_in = {k: v for k, v in _L0_gnn_all.items() if k in ('W', 'b')}
    del _L0_gnn_all

    def _L1_gnn_setup():
        import jax, jax.numpy as jnp
        import numpy as np
        N = 12500
        E = 200000
        IN = 128
        H = 4
        C = 32
        NEG_SLOPE = 0.2
        key = jax.random.key(seed)
        ks = jax.random.split(key, 10)
        feats = jax.random.normal(ks[0], (N, IN), dtype=jnp.float32)
        src = jax.random.randint(ks[1], (E,), 0, N)
        off = jax.random.randint(ks[2], (E,), 1, N)
        dst = (src + off) % N
        edge_index = jnp.stack([src, dst]).astype(jnp.int64)
        scale = 1.0 / np.sqrt(IN)
        W_src = jax.random.uniform(ks[3], (H * C, IN), jnp.float32, -scale, scale)
        W_res = jax.random.uniform(ks[4], (H * C, IN), jnp.float32, -scale, scale)
        att_src = jax.random.normal(ks[5], (1, H, C), dtype=jnp.float32) * 0.1
        att_dst = jax.random.normal(ks[6], (1, H, C), dtype=jnp.float32) * 0.1
        bias = jnp.zeros((H * C,), dtype=jnp.float32)
        gamma = jnp.ones((H * C,), dtype=jnp.float32)
        beta = jnp.zeros((H * C,), dtype=jnp.float32)
        return {'feats': feats, 'edge_index': edge_index, 'W_src': W_src, 'att_src': att_src, 'att_dst': att_dst, 'W_res': W_res, 'bias': bias, 'gamma': gamma, 'beta': beta}
    _L1_gnn_all = _L1_gnn_setup()
    _L1_gnn_in = {k: v for k, v in _L1_gnn_all.items() if k in ('W_src', 'att_src', 'att_dst', 'W_res', 'bias', 'gamma', 'beta')}
    del _L1_gnn_all

    def _L2_gnn_setup():
        import jax, jax.numpy as jnp
        import numpy as np
        N_ENT = 2048
        N_REL = 50
        D = 128
        B = 4
        E = 32768
        key = jax.random.key(seed)
        k1, k2, k3, k4, k5, k6 = jax.random.split(key, 6)
        x = jax.random.normal(k1, (N_ENT, D), dtype=jnp.float32)
        bases = jax.random.normal(k2, (B, D, D), dtype=jnp.float32) * 0.05
        comps = jax.random.normal(k3, (N_REL, B), dtype=jnp.float32)
        alpha = jax.random.normal(k4, (N_REL, 1), dtype=jnp.float32)
        edge_index = jax.random.randint(k5, (2, E), 0, N_ENT, dtype=jnp.int64)
        edge_type = jax.random.randint(k6, (E,), 0, N_REL, dtype=jnp.int64)
        return {'x': x, 'bases': bases, 'comps': comps, 'alpha': alpha, 'edge_index': edge_index, 'edge_type': edge_type}
    _L2_gnn_all = _L2_gnn_setup()
    _L2_gnn_in = {k: v for k, v in _L2_gnn_all.items() if k in ('bases', 'comps', 'alpha')}
    del _L2_gnn_all

    def _L3_gnn_setup():
        import jax, jax.numpy as jnp
        import numpy as np
        N = 5000
        E = 80000
        CIN = 128
        COUT = 128
        EDGE_DIM = 2
        BN_EPS = 1e-05
        key = jax.random.key(seed)
        ks = jax.random.split(key, 9)
        din = 2 * CIN + EDGE_DIM
        x = jax.random.normal(ks[0], (N, CIN), dtype=jnp.float32)
        edge_index = jax.random.randint(ks[1], (2, E), 0, N, dtype=jnp.int64)
        edge_attr = jax.random.normal(ks[2], (E, EDGE_DIM), dtype=jnp.float32)
        W1 = jax.random.normal(ks[3], (din, COUT), dtype=jnp.float32) / np.sqrt(din)
        b1 = jax.random.normal(ks[4], (COUT,), dtype=jnp.float32) * 0.01
        gamma = jnp.ones((COUT,), dtype=jnp.float32)
        beta = jnp.zeros((COUT,), dtype=jnp.float32)
        W2 = jax.random.normal(ks[5], (COUT, COUT), dtype=jnp.float32) / np.sqrt(COUT)
        b2 = jax.random.normal(ks[6], (COUT,), dtype=jnp.float32) * 0.01
        return {'x': x, 'edge_index': edge_index, 'edge_attr': edge_attr, 'W1': W1, 'b1': b1, 'gamma': gamma, 'beta': beta, 'W2': W2, 'b2': b2}
    _L3_gnn_all = _L3_gnn_setup()
    _L3_gnn_in = {k: v for k, v in _L3_gnn_all.items() if k in ('W1', 'b1', 'gamma', 'beta', 'W2', 'b2')}
    del _L3_gnn_all
    return {'x': x, 'src': src, 'dst': dst, 'edge_attr_2': edge_attr_2, 'edge_type_50': edge_type_50, 'L0_gnn_W': _L0_gnn_in['W'], 'L0_gnn_b': _L0_gnn_in['b'], 'L1_gnn_W_src': _L1_gnn_in['W_src'], 'L1_gnn_att_src': _L1_gnn_in['att_src'], 'L1_gnn_att_dst': _L1_gnn_in['att_dst'], 'L1_gnn_W_res': _L1_gnn_in['W_res'], 'L1_gnn_bias': _L1_gnn_in['bias'], 'L1_gnn_gamma': _L1_gnn_in['gamma'], 'L1_gnn_beta': _L1_gnn_in['beta'], 'L2_gnn_bases': _L2_gnn_in['bases'], 'L2_gnn_comps': _L2_gnn_in['comps'], 'L2_gnn_alpha': _L2_gnn_in['alpha'], 'L3_gnn_W1': _L3_gnn_in['W1'], 'L3_gnn_b1': _L3_gnn_in['b1'], 'L3_gnn_gamma': _L3_gnn_in['gamma'], 'L3_gnn_beta': _L3_gnn_in['beta'], 'L3_gnn_W2': _L3_gnn_in['W2'], 'L3_gnn_b2': _L3_gnn_in['b2']}

def reference(x, src, dst, edge_attr_2, edge_type_50, L0_gnn_W, L0_gnn_b, L1_gnn_W_src, L1_gnn_att_src, L1_gnn_att_dst, L1_gnn_W_res, L1_gnn_bias, L1_gnn_gamma, L1_gnn_beta, L2_gnn_bases, L2_gnn_comps, L2_gnn_alpha, L3_gnn_W1, L3_gnn_b1, L3_gnn_gamma, L3_gnn_beta, L3_gnn_W2, L3_gnn_b2):
    import jax
    import jax.numpy as jnp

    def _L0_gnn_ref(x, edge_index, W, b):
        import jax, jax.numpy as jnp
        import numpy as np
        N_NODES = 6250
        IN_CH = 128
        OUT_CH = 128
        N_EDGES = 80000
        src, dst = (edge_index[0], edge_index[1])
        neighbor_sum = jax.ops.segment_sum(x[src], dst, num_segments=x.shape[0])
        neighbor_count = jax.ops.segment_sum(jnp.ones((src.shape[0],), dtype=x.dtype), dst, num_segments=x.shape[0])
        neighbor_mean = neighbor_sum / jnp.clip(neighbor_count, 1.0)[:, None]
        h = jnp.concatenate([x, neighbor_mean], axis=-1)
        return h @ W.T + b

    def _L1_gnn_ref(feats, edge_index, W_src, att_src, att_dst, W_res, bias, gamma, beta):
        import jax, jax.numpy as jnp
        import numpy as np
        N = 12500
        E = 200000
        IN = 128
        H = 4
        C = 32
        NEG_SLOPE = 0.2
        n = feats.shape[0]
        loop = jnp.arange(n)
        src = jnp.concatenate([edge_index[0], loop])
        dst = jnp.concatenate([edge_index[1], loop])
        xp = (feats @ W_src.T).reshape(n, H, C)
        a_src = jnp.sum(xp * att_src, axis=-1)
        a_dst = jnp.sum(xp * att_dst, axis=-1)
        e = jax.nn.leaky_relu(a_src[src] + a_dst[dst], NEG_SLOPE)
        m = jax.ops.segment_max(e, dst, num_segments=n)
        ex = jnp.exp(e - m[dst])
        s = jax.ops.segment_sum(ex, dst, num_segments=n)
        alpha = ex / (s[dst] + 1e-16)
        msg = alpha[:, :, None] * xp[src]
        out = jax.ops.segment_sum(msg, dst, num_segments=n)
        res = (feats @ W_res.T).reshape(n, H, C)
        out = out + res + bias.reshape(1, H, C)
        out = out.reshape(n, H * C)
        mu = out.mean(axis=0)
        var = jnp.mean((out - mu) ** 2, axis=0)
        return (out - mu) / jnp.sqrt(var + 1e-05) * gamma + beta

    def _L2_gnn_ref(x, bases, comps, alpha, edge_index, edge_type):
        import jax, jax.numpy as jnp
        import numpy as np
        N_ENT = 2048
        N_REL = 50
        D = 128
        B = 4
        E = 32768
        n = x.shape[0]
        row, col = (edge_index[0], edge_index[1])
        ones = jnp.ones(row.shape, x.dtype)
        deg = jax.ops.segment_sum(ones, row, num_segments=n)
        deg_inv = jnp.where(deg > 0, jax.lax.rsqrt(jnp.maximum(deg, 1.0)), 0.0)
        norm = deg_inv[row] * deg_inv[col]
        h_j = x[col]
        c_e = comps[edge_type]
        hj_b = c_e[:, :, None] * h_j[:, None, :]
        msg = jnp.einsum('ebd,bdf->ef', hj_b, bases)
        msg = msg * alpha[edge_type] * norm[:, None]
        out = jax.ops.segment_sum(msg, row, num_segments=n)
        return out

    def _L3_gnn_ref(x, edge_index, edge_attr, W1, b1, gamma, beta, W2, b2):
        import jax, jax.numpy as jnp
        import numpy as np
        N = 5000
        E = 80000
        CIN = 128
        COUT = 128
        EDGE_DIM = 2
        BN_EPS = 1e-05
        n_nodes = x.shape[0]
        row, col = (edge_index[0], edge_index[1])
        ef = jnp.concatenate([x[row], x[col], edge_attr], axis=-1)
        h = ef @ W1 + b1
        mu = jnp.mean(h, axis=0)
        var = jnp.mean((h - mu) ** 2, axis=0)
        h = (h - mu) * jax.lax.rsqrt(var + BN_EPS) * gamma + beta
        h = jax.nn.relu(h)
        msgs = h @ W2 + b2
        sums = jax.ops.segment_sum(msgs, row, num_segments=n_nodes)
        counts = jax.ops.segment_sum(jnp.ones((msgs.shape[0],), dtype=msgs.dtype), row, num_segments=n_nodes)
        out = sums / (counts + 1.0)[:, None]
        return out + x
    edge_index = jnp.stack([src, dst])
    x = _layernorm(x + _L0_gnn_ref(x, edge_index, L0_gnn_W, L0_gnn_b), axis=-1)
    x = _layernorm(x + _L1_gnn_ref(x, edge_index, L1_gnn_W_src, L1_gnn_att_src, L1_gnn_att_dst, L1_gnn_W_res, L1_gnn_bias, L1_gnn_gamma, L1_gnn_beta), axis=-1)
    x = _layernorm(x + _L2_gnn_ref(x, L2_gnn_bases, L2_gnn_comps, L2_gnn_alpha, edge_index, edge_type_50), axis=-1)
    x = _layernorm(x + _L3_gnn_ref(x, edge_index, edge_attr_2, L3_gnn_W1, L3_gnn_b1, L3_gnn_gamma, L3_gnn_beta, L3_gnn_W2, L3_gnn_b2), axis=-1)
    return x

_drawn_inputs = setup_inputs


def setup_inputs(seed=0):
    import zlib

    import numpy as np

    out = dict(_drawn_inputs(seed))
    spreads = {'L1_gnn_bias': (0.0, 0.8),
     'L1_gnn_gamma': (1.0, 0.2),
     'L1_gnn_beta': (0.0, 0.1),
     'L3_gnn_gamma': (1.0, 0.2),
     'L3_gnn_beta': (0.0, 0.353)}
    factors = {'edge_attr_2': 8.0, 'L1_gnn_att_dst': 3.619, 'L3_gnn_b1': 8.0, 'L3_gnn_b2': 8.0}
    for name, (base, spread) in spreads.items():
        noise = np.random.default_rng([zlib.crc32(name.encode()), seed]).standard_normal(out[name].shape)
        drawn = base * np.exp(spread * noise) if base else spread * noise
        out[name] = jnp.asarray(drawn.astype(out[name].dtype))
    for name, factor in factors.items():
        out[name] = (out[name] * factor).astype(out[name].dtype)
    return out
```

```python
from contextlib import ExitStack

import concourse.bass as bass
from concourse import mybir

ALU = mybir.AluOpType
ACT = mybir.ActivationFunctionType
AX_X = mybir.AxisListType.X
F32 = mybir.dt.float32
I32 = mybir.dt.int32
U16 = mybir.dt.uint16
ds = bass.ds

P = 128
TILE_SHIFT = 7
FEAT = 128
HEADS = 4
CH = FEAT // HEADS
GROUP = 4
RING = 4
EPS = 1e-5
ABSENT = 1e30


def gnn_program(nc, x, src, dst, edge_attr, edge_type, L0_W, L0_b, L1_W_src, L1_att_src, L1_att_dst,
                L1_W_res, L1_bias, L1_gamma, L1_beta, L2_bases, L2_comps, L2_alpha, L3_W1, L3_b1,
                L3_gamma, L3_beta, L3_W2, L3_b2, out):
    N = x.shape[0]
    E = src.shape[0]
    TILES = -(-N // P)
    BUCKETS = TILES + 1
    LAST = N - (TILES - 1) * P
    COLS = -(-E // P)
    FULL = E // COLS
    REST = E - FULL * COLS
    PAD_NODE = TILES * P
    NODES = BUCKETS * P
    CHUNKS = (COLS * P + BUCKETS * (P - 1)) // P
    CHUNKS = -(-CHUNKS // P) * P
    MAPC = CHUNKS // P
    GROUPS = CHUNKS // GROUP
    NAT_GROUPS = COLS // GROUP
    assert COLS % GROUP == 0 and FULL == P - 1
    RELS, BASES = L2_comps.shape
    DREC = 2
    SREC = 8
    ROW = FEAT + HEADS
    SCORES = 3 * HEADS

    def dram(name, shape, dt=F32):
        return nc.dram_tensor(name, shape, dt).ap()

    recD_dram = dram("rec_by_dst", (P * CHUNKS, DREC))
    recS_dram = dram("rec_by_src", (P * CHUNKS, SREC))
    mapD_dram = dram("tile_of_dst_chunk", (CHUNKS,), U16)
    mapS_dram = dram("tile_of_src_chunk", (CHUNKS,), U16)
    x_table = dram("x_table", (NODES, FEAT))
    score_table = dram("score_table", (NODES, HEADS))
    xp_table = dram("xp_table", (NODES, FEAT))
    y_table = dram("y_table", (NODES, FEAT))
    q_table = dram("q_table", (NODES, FEAT))
    hidden = dram("hidden", (P, CHUNKS, FEAT))

    with ExitStack() as ctx:
        def sb(name, shape, dt=F32):
            return ctx.enter_context(nc.sbuf_tensor(name, shape, dt))[:]

        sem_names = []

        def sem(name):
            sem_names.append(name)
            return ctx.enter_context(nc.semaphore(name))

        NAT = 21 * COLS
        LAYERS = BUCKETS * FEAT * (1 + BASES)
        region = sb("region", [P, max(NAT, LAYERS)])
        nat = [region[:, n * COLS:(n + 1) * COLS] for n in range(21)]
        key_d, key_s, kind = (a.bitcast(I32) for a in nat[0:3])
        attr_in = region[:, 3 * COLS:5 * COLS].rearrange("p (c k) -> p c k", k=2)
        tile_f, mask, cum, pos_f = nat[5:9]
        pos_d, pos_s = nat[9].bitcast(I32), nat[10].bitcast(I32)
        natD = region[:, 11 * COLS:13 * COLS].rearrange("p (c k) -> p c k", k=DREC)
        natS = region[:, 13 * COLS:21 * COLS].rearrange("p (c k) -> p c k", k=SREC)
        at = BUCKETS * FEAT
        X = region[:, 0:at].rearrange("p (t f) -> p t f", f=FEAT)
        acc_flat = region[:, at:at + BUCKETS * ROW]
        acc = acc_flat.rearrange("p (t f) -> p t f", f=ROW)
        ln_tmp = region[:, at:at + TILES * FEAT].rearrange("p (t f) -> p t f", f=FEAT)
        rel_flat = region[:, at:at + BUCKETS * BASES * FEAT]
        rel_acc = rel_flat.rearrange("p (t f) -> p t f", f=BASES * FEAT)
        at += BUCKETS * ROW
        edge_score = region[:, at:at + CHUNKS * HEADS].rearrange("p (c h) -> p c h", h=HEADS)
        squares = region[:, at:at + TILES * FEAT].rearrange("p (t f) -> p t f", f=FEAT)
        Pt_flat = region[:, at:at + BUCKETS * FEAT]
        Pt = Pt_flat.rearrange("p (t f) -> p t f", f=FEAT)
        at += BUCKETS * FEAT
        weighted_pq = region[:, at:at + TILES * FEAT].rearrange("p (t f) -> p t f", f=FEAT)

        at += TILES * FEAT
        weighted_q = region[:, at:at + TILES * FEAT].rearrange("p (t f) -> p t f", f=FEAT)

        G = sb("gathered", [P, RING, GROUP, ROW])
        hot = sb("hot", [P, RING, GROUP, P])
        hotT = sb("hotT", [P, 2, GROUP, P])
        wide = sb("wide", [P, RING, GROUP, P])
        sq = sb("sq", [P, 2, GROUP, P])
        stD = sb("staged_dst", [P, RING, GROUP, DREC])
        stS = sb("staged_src", [P, RING, GROUP, SREC])
        stP = sb("staged_pos", [P, RING, GROUP], I32)
        mapD = sb("map_dst", [1, CHUNKS], U16)
        mapS = sb("map_src", [1, CHUNKS], U16)
        iota = sb("iota", [P, P])
        diff = sb("diff", [P, P])
        ident = sb("ident", [P, P])
        upper = sb("upper", [P, P])
        ones = sb("ones", [P, P])
        zeros = sb("zeros", [P, P])
        chunk_id = sb("chunk_id", [P, MAPC])
        cnt = sb("cnt", [P, BUCKETS])
        size = sb("size", [P, BUCKETS])
        size_i = sb("size_i", [P, BUCKETS], I32)
        ends = sb("ends", [P, BUCKETS])
        base = sb("base", [P, BUCKETS])
        is_past = sb("is_past", [P, MAPC, BUCKETS])
        map_f = sb("map_f", [P, MAPC])
        mapU = [sb("map_u_dst", [P, MAPC], U16), sb("map_u_src", [P, MAPC], U16)]
        comps = sb("comps", [P, RELS, BASES])
        alpha = sb("alpha", [P, RELS])
        attr_sum = sb("attr_sum", [P, 2])
        degs = sb("degs", [P, BUCKETS, 2])
        dinv = sb("dinv", [P, BUCKETS])
        col = sb("col", [P, BUCKETS])
        col2 = sb("col2", [P, BUCKETS])
        root = sb("root", [P, P])
        att = sb("att", [P, BUCKETS, SCORES])
        selfw = sb("selfw", [P, BUCKETS, HEADS])
        selfw2 = sb("selfw2", [P, BUCKETS, HEADS])
        chunk_max = sb("chunk_max", [P, 2, GROUP, HEADS])
        e_sum = sb("e_sum", [P, 2, GROUP, HEADS])
        e_lrelu = sb("e_lrelu", [P, 2, GROUP, HEADS])
        e_arg = sb("e_arg", [P, 2, GROUP, HEADS])
        raw = sb("raw", [P, 4, FEAT])
        blockdiag = sb("blockdiag", [P, SCORES])
        attcol = sb("attcol", [P, 2])
        W0 = sb("W0", [P, 2, FEAT])
        W_src = sb("W_src", [P, FEAT + SCORES])
        W_res = sb("W_res", [P, FEAT])
        bases = sb("bases", [P, BASES, FEAT])
        W1 = sb("W1", [P, 2, FEAT])
        W2 = sb("W2", [P, FEAT])
        row_names = ["b0", "bias1", "gamma1", "beta1", "b1", "w_attr0", "w_attr1", "gamma3", "beta3", "b2"]
        rows = {n: sb("row_" + n, [P, FEAT]) for n in row_names}
        mean_row = sb("mean_row", [P, FEAT])
        scale_row = sb("scale_row", [P, FEAT])
        attr_mean = sb("attr_mean", [P, 2])
        sel = sb("sel", [GROUP * SREC, GROUP, FEAT])
        recT = sb("recT", [GROUP * SREC, 2, P])
        xs = sb("tile_fetched", [P, BASES, P])
        xT = sb("tile_turned", [P, 2, P])

        banks = [ctx.enter_context(nc.psum_tensor(f"bank{i}", [P, 512], F32))[:] for i in range(8)]

        padD = hot.rearrange("p q u n -> p (q u n)")
        padS = hotT.rearrange("p q u n -> p (q u n)")
        PAD_D_COLS = RING * GROUP * P // DREC
        PAD_S_COLS = 2 * GROUP * P // SREC
        FILLS = -(-CHUNKS // PAD_D_COLS) + -(-CHUNKS // PAD_S_COLS)
        ROWS_LOADED = 10
        WLOADS = 10 + ROWS_LOADED + GROUP
        NAT_ROUNDS = [-(-(NAT_GROUPS - q) // RING) for q in range(RING)]

        def scatter_out(q, u, width):
            return banks[2 * (q % 2) + u // 2][:, (u % 2) * ROW:(u % 2) * ROW + width]

        s_const = sem("const_ready")
        s_setup = sem("setup_steps")
        s_keys = sem("keys_loaded")
        s_kinds = sem("kinds_loaded")
        s_wload = sem("weights_loaded")
        s_x = sem("x_loaded")
        s_xpad = sem("x_pad_rows_zeroed")
        s_seen = sem("vector_seen")
        s_fill = sem("records_filled")
        s_table0 = sem("tables_zeroed")
        s_step = sem("vector_steps")
        s_cnt = sem("bucket_counts")
        s_rank = sem("rank_steps")
        s_coef = sem("coef_steps")
        s_prefix_in = sem("prefix_in")
        s_prefix_out = sem("prefix_out")
        s_nat = [sem("nat_by_dst_ready"), sem("nat_by_src_ready")]
        s_mapped = sem("maps_stored")
        s_maps = sem("maps_loaded")
        s_nstage = [[sem(f"nat_staged_{w}{q}") for q in range(RING)] for w in range(2)]
        s_nscat = [[sem(f"nat_scattered_{w}{q}") for q in range(RING)] for w in range(2)]
        s_go = sem("pool_go")
        s_root_in = sem("root_in")
        s_root_out = sem("root_out")
        s_w_tr = sem("weights_transposed")
        s_w_copied = sem("weights_copied")

        presets = []

        class Pass:

            def __init__(self, name, has, before, loads=1, gathers=True):
                def s(what):
                    return sem(f"{name}_{what}") if what in has.split() else None
                self.loads = loads
                self.staged0 = before.staged1 if before else 0
                self.gathered0 = before.gathered1 if before else 0
                self.staged1 = self.staged0 + 16 * loads * (GROUPS // RING)
                self.gathered1 = self.gathered0 + (16 * GROUPS if gathers else 0)
                self.hot = s("hot")
                self.turned = s("turned")
                self.hotT = s("hotT")
                self.spread = s("spread")
                self.used = s("used")
                self.weighted = s("weighted")
                self.scaled = s("scaled")
                self.summed = s("summed")
                self.added = sem(f"{name}_added")
                presets.append((self.added, GROUP * RING))

            def staged(self, i):
                return i * (16 * self.loads) + (16 * self.loads + self.staged0)

            def gathered(self, i):
                return i * (16 * GROUP) + (16 * GROUP + self.gathered0)

        class NodeLoop:

            def __init__(self, name):
                def s(what):
                    return sem(f"{name}_{what}")
                self.start = s("start")
                self.fetched = s("fetched")
                self.turned = s("turned")
                self.copied = s("copied")
                self.product = s("product")
                self.taken = s("taken")
                self.taken2 = s("taken2") if name in ("n1a", "n3a", "n3b") else None
                presets.append((self.taken, 1))

        def when(i, q, more=0):
            return 4 * i + (q + more)

        def pipeline(eng, stages, groups=GROUPS):
            ahead = max(lead for _, lead in stages)
            first = RING
            last = (groups - ahead) // RING

            def step(i, q):
                for f, lead in stages:
                    g = q + lead
                    if isinstance(i, int):
                        if 0 <= RING * i + g < groups:
                            f((RING * i + g) // RING, g % RING)
                    else:
                        f(i + g // RING if g >= RING else i, g % RING)

            for s in range(-ahead, first):
                step(s // RING, s % RING)
            with eng.Fori(first // RING, last) as i:
                for q in range(RING):
                    step(i, q)
            for s in range(last * RING, groups):
                step(s // RING, s % RING)

        s_staged = [sem(f"records_staged{q}") for q in range(RING)]
        s_gathered = [sem(f"rows_gathered{q}") for q in range(RING)]
        p0 = Pass("l0", "hot used summed", None, loads=2)
        p1a = Pass("l1a", "hot turned hotT spread used weighted", p0)
        p1b = Pass("l1b", "hot turned hotT spread used weighted scaled summed", p1a)
        p2 = Pass("l2", "hot scaled used", p1b)
        p3a = Pass("l3a", "hot turned hotT summed", p2)
        p3b = Pass("l3b", "hot used scaled weighted summed", p3a, gathers=False)
        s_deg = sem("l0_deg_added")
        s_hotS = sem("l0_hot_src")
        s_self = sem("l1_self_arg")
        s_selfexp = sem("l1_self_exp")
        s_exp = sem("l1b_exp")
        s_recT = sem("l3a_records_turned")
        s_recTc = sem("l3a_records_copied")
        s_square = sem("l3a_squares")
        s_sqsum = sem("l3a_squares_summed")
        s_hstored = [sem(f"l3a_hidden_stored{q}") for q in range(RING)]
        s_hload = [sem(f"l3b_hidden_loaded{q}") for q in range(RING)]
        for s in s_hstored:
            presets.append((s, 16))
        for ps in (p0, p1b, p3a, p3b):
            presets.append((ps.summed, RING))
        for ps in (p1a, p3a):
            presets.append((ps.turned, RING))
        for ps in (p1a, p1b, p3a):
            presets.append((ps.hotT, 2))
        presets += [(p0.used, RING), (s_deg, GROUP * RING), (p1b.spread, 2), (p1b.used, 2), (s_exp, 2),
                    (p2.used, GROUP), (p2.scaled, GROUP * RING), (s_recTc, 2), (s_square, RING), (s_sqsum, 2)]
        n0, n1a, n1b, n2, n3a, n3b = (NodeLoop(n) for n in ("n0", "n1a", "n1b", "n2", "n3a", "n3b"))
        s_bn_in = sem("bn_in")
        s_bn_out = sem("bn_out")
        s_tables = sem("tables_ready")
        s_stored = sem("tables_stored")
        s_mu_in = sem("mu_in")
        s_mu = sem("mu_out")
        s_final = sem("final_ready")
        s_out = sem("out_stored")

        def offset(ap):
            return bass.IndirectOffsetOnAxis(ap=ap, axis=0)

        block = ctx.enter_context(nc.Block())

        @block.sync
        def _(sp):
            def load_by_partition(flat, width, to, done):
                body = flat[0:FULL * COLS * width].rearrange("(p n) -> p n", p=FULL)
                most = FULL // 16 * 16
                sp.dma_start(to[0:most], body[0:most]).then_inc(done, 16)
                sp.dma_start(to[most:FULL], body[most:FULL]).then_inc(done, 16)
                sp.dma_start(to[FULL:FULL + 1, 0:REST * width],
                             flat[FULL * COLS * width:].rearrange("(p n) -> p n", p=1)).then_inc(done, 16)

            sp.wait_ge(s_setup, 1)
            load_by_partition(dst, 1, key_d, s_keys)
            load_by_partition(src, 1, key_s, s_keys)
            load_by_partition(edge_type, 1, kind, s_kinds)
            load_by_partition(edge_attr.rearrange("e k -> (e k)"), 2, region[:, 3 * COLS:5 * COLS], s_kinds)
            sp.dma_start(comps.rearrange("p r b -> p (r b)"),
                         L2_comps.rearrange("r b -> (r b)").partition_broadcast(P)).then_inc(s_wload, 16)
            sp.dma_start(alpha, L2_alpha.rearrange("r a -> (r a)").partition_broadcast(P)).then_inc(s_wload, 16)
            sp.dma_start(raw[:, 0:2, :], L0_W.rearrange("o (k f) -> o k f", k=2)).then_inc(s_wload, 16)
            sp.dma_start(raw[:, 2, :], L1_W_src).then_inc(s_wload, 16)
            sp.dma_start(raw[:, 3, :], L1_W_res).then_inc(s_wload, 16)
            with nc.allow_non_contiguous_dma(reason="one column of 128 values"):
                sp.dma_start(attcol[:, 0:1], L1_att_dst.rearrange("a h c -> (h c) a")).then_inc(s_wload, 16)
                sp.dma_start(attcol[:, 1:2], L1_att_src.rearrange("a h c -> (h c) a")).then_inc(s_wload, 16)
            sp.dma_start(bases, L2_bases.rearrange("b d f -> d b f")).then_inc(s_wload, 16)
            sp.dma_start(W1, L3_W1[0:2 * FEAT, :].rearrange("(k d) f -> d k f", k=2)).then_inc(s_wload, 16)
            sp.dma_start(W2, L3_W2).then_inc(s_wload, 16)
            row_src = {"b0": L0_b, "bias1": L1_bias, "gamma1": L1_gamma, "beta1": L1_beta, "b1": L3_b1,
                       "w_attr0": L3_W1[2 * FEAT, :], "w_attr1": L3_W1[2 * FEAT + 1, :],
                       "gamma3": L3_gamma, "beta3": L3_beta, "b2": L3_b2}
            for n in row_names:
                sp.dma_start(rows[n], row_src[n].partition_broadcast(P)).then_inc(s_wload, 16)
            for u in range(GROUP):
                r = u * SREC + 2
                sp.dma_start(sel[r:r + 2, u, :], L3_W1[2 * FEAT:2 * FEAT + 2, :]).then_inc(s_wload, 16)
            for c0 in range(0, CHUNKS, PAD_S_COLS):
                c1 = min(CHUNKS, c0 + PAD_S_COLS)
                sp.dma_start(recS_dram.rearrange("(p c) k -> p (c k)", p=P)[:, c0 * SREC:c1 * SREC],
                             padS[:, 0:(c1 - c0) * SREC]).then_inc(s_fill, 16)
            for c0 in range(0, CHUNKS, PAD_D_COLS):
                c1 = min(CHUNKS, c0 + PAD_D_COLS)
                sp.dma_start(recD_dram.rearrange("(p c) k -> p (c k)", p=P)[:, c0 * DREC:c1 * DREC],
                             padD[:, 0:(c1 - c0) * DREC]).then_inc(s_fill, 16)
            sp.dma_start(x_table[0:N, :], x).then_inc(s_table0, 16)
            sp.dma_start(x_table[N:PAD_NODE, :], zeros[0:PAD_NODE - N, :]).then_inc(s_table0, 16)
            for table in (x_table, xp_table, y_table, q_table):
                sp.dma_start(table[PAD_NODE:NODES, :], zeros).then_inc(s_table0, 16)
            sp.dma_start(score_table[PAD_NODE:NODES, :], zeros[:, 0:HEADS]).then_inc(s_table0, 16)

            for w, (rec, st, pos) in enumerate(((natD, stD, pos_d), (natS, stS, pos_s))):
                sp.wait_ge(s_nat[w], 1)
                if w == 0:
                    sp.wait_ge(s_fill, 16 * FILLS)

                def stage(i, q, first=False):
                    if not first:
                        sp.wait_ge(s_nscat[w][q], 64 * i)
                    sp.dma_start(st[:, q], rec[:, ds(16 * i + 4 * q, 4), :]).then_inc(s_nstage[w][q], 16)
                    sp.dma_start(stP[:, q], pos[:, ds(16 * i + 4 * q, 4)]).then_inc(s_nstage[w][q], 16)

                if w == 1:
                    for q in range(RING):
                        sp.wait_ge(s_nscat[0][q], 64 * NAT_ROUNDS[q])
                for q in range(RING):
                    stage(0, q, first=True)
                with sp.Fori(1, NAT_GROUPS // RING) as i:
                    for q in range(RING):
                        stage(i, q)
                for q in range(NAT_GROUPS % RING):
                    stage(NAT_GROUPS // RING, q)

            sp.wait_ge(s_nat[1], 1)
            sp.dma_start(mapD_dram.rearrange("(p c) -> p c", p=P), mapU[0]).then_inc(s_mapped, 16)
            sp.dma_start(mapS_dram.rearrange("(p c) -> p c", p=P), mapU[1]).then_inc(s_mapped, 16)
            sp.wait_ge(s_mapped, 32)
            sp.dma_start(mapD, mapD_dram.rearrange("(a c) -> a c", a=1)).then_inc(s_maps, 16)
            sp.dma_start(mapS, mapS_dram.rearrange("(a c) -> a c", a=1)).then_inc(s_maps, 16)
            for w in range(2):
                for q in range(RING):
                    sp.wait_ge(s_nscat[w][q], 64 * NAT_ROUNDS[q])
            sp.dma_start(X[:, 0:TILES - 1, :], x[0:(TILES - 1) * P, :].rearrange("(t p) f -> p t f", p=P)).then_inc(s_x, 16)
            sp.wait_ge(s_xpad, 1)
            sp.dma_start(X[0:LAST, TILES - 1, :], x[(TILES - 1) * P:N, :]).then_inc(s_x, 16)
            sp.wait_ge(s_table0, 16 * 7)

            recD_view = recD_dram.rearrange("(p c) k -> p c k", p=P)
            recS_view = recS_dram.rearrange("(p c) k -> p c k", p=P)

            def stage_records(ps, streams):
                def stage(i, q):
                    sp.wait_ge(ps.added, 16 * i + 4 * q + 4)
                    for st, view in streams:
                        sp.dma_start(st[:, q], view[:, ds(16 * i + 4 * q, 4), :]).then_inc(s_staged[q], 16)
                with sp.Fori(0, GROUPS // RING) as i:
                    for q in range(RING):
                        stage(i, q)

            stage_records(p0, [(stD, recD_view), (stS, recS_view)])
            sp.wait_ge(s_tables, 1)
            sp.dma_start(xp_table[0:PAD_NODE, :].rearrange("(t p) f -> p t f", p=P),
                         acc[:, 0:TILES, 0:FEAT]).then_inc(s_stored, 16)
            sp.dma_start(score_table[0:PAD_NODE, :].rearrange("(t p) f -> p t f", p=P),
                         att[:, 0:TILES, 2 * HEADS:SCORES]).then_inc(s_stored, 16)
            sp.wait_ge(s_stored, 32)
            stage_records(p1a, [(stD, recD_view)])
            sp.wait_ge(p1a.added, 4 * GROUPS + 16)
            stage_records(p1b, [(stD, recD_view)])
            sp.wait_ge(s_tables, 2)
            sp.dma_start(y_table[0:PAD_NODE, :].rearrange("(t p) f -> p t f", p=P), ln_tmp).then_inc(s_stored, 16)
            sp.wait_ge(s_stored, 48)
            stage_records(p2, [(stS, recS_view)])
            sp.wait_ge(s_tables, 3)
            sp.dma_start(q_table[0:PAD_NODE, :].rearrange("(t p) f -> p t f", p=P),
                         acc[:, 0:TILES, 0:FEAT]).then_inc(s_stored, 16)
            sp.wait_ge(s_stored, 64)
            stage_records(p3a, [(stS, recS_view)])
            sp.wait_ge(s_square, GROUPS + RING)
            for q in range(RING):
                sp.wait_ge(s_hstored[q], 16 * (GROUPS // RING) + 16)

            def load_hidden(i, q):
                sp.wait_ge(p3b.added, 16 * i + 4 * q + 4)
                sp.dma_start(wide[:, q], hidden[:, ds(16 * i + 4 * q, 4), :]).then_inc(s_hload[q], 16)
                sp.dma_start(stS[:, q], recS_view[:, ds(16 * i + 4 * q, 4), :]).then_inc(s_staged[q], 16)
            with sp.Fori(0, GROUPS // RING) as i:
                for q in range(RING):
                    load_hidden(i, q)
            sp.wait_ge(s_final, 1)
            sp.dma_start(out[0:(TILES - 1) * P, :].rearrange("(t p) f -> p t f", p=P), X[:, 0:TILES - 1, :]).then_inc(s_out, 16)
            sp.dma_start(out[(TILES - 1) * P:N, :], X[0:LAST, TILES - 1, :]).then_inc(s_out, 16)
            sp.wait_ge(s_out, 32)

        @block.gpsimd
        def _(pool):
            pool.iota(iota, [[1, P]], base=0, channel_multiplier=0,
                      allow_small_or_imprecise_dtypes=True).then_inc(s_const, 1)
            pool.iota(diff, [[1, P]], base=0, channel_multiplier=-1,
                      allow_small_or_imprecise_dtypes=True).then_inc(s_const, 1)
            pool.iota(chunk_id, [[1, MAPC]], base=0, channel_multiplier=MAPC,
                      allow_small_or_imprecise_dtypes=True).then_inc(s_const, 1)

            for w, (st, table, width) in enumerate(((stD, recD_dram, DREC), (stS, recS_dram, SREC))):
                def scatter(i, q):
                    pool.wait_ge(s_nstage[w][q], 32 * i + 32)
                    pool.sem_inc(s_go, 1)
                    for u in range(GROUP):
                        pool.indirect_dma_start(out=table, out_offset=offset(stP[:, q, u:u + 1]),
                                                in_=st[:, q, u, :], in_offset=None).then_inc(s_nscat[w][q], 16)
                with pool.Fori(0, NAT_GROUPS // RING) as i:
                    for q in range(RING):
                        scatter(i, q)
                for q in range(NAT_GROUPS % RING):
                    scatter(NAT_GROUPS // RING, q)

            def gather_rows(ps, st, table, width):
                def gather(i, q):
                    pool.wait_ge(s_staged[q], ps.staged(i))
                    pool.sem_inc(s_go, 1)
                    for u in range(GROUP):
                        pool.indirect_dma_start(out=G[:, q, u, 0:width], out_offset=None, in_=table,
                                                in_offset=offset(st[:, q, u, 0:1].bitcast(I32))
                                                ).then_inc(s_gathered[q], 16)
                with pool.Fori(0, GROUPS // RING) as i:
                    for q in range(RING):
                        gather(i, q)

            gather_rows(p0, stD, x_table, FEAT)
            gather_rows(p1a, stD, score_table, HEADS)
            gather_rows(p1b, stD, xp_table, FEAT)
            gather_rows(p2, stS, y_table, FEAT)
            gather_rows(p3a, stS, q_table, FEAT)

        @block.scalar
        def _(act):
            roots = [0]

            def take_root(width):
                roots[0] += 1
                act.wait_ge(s_root_in, roots[0])
                act.activation(root[:, 0:width], root[:, 0:width], ACT.Sqrt).then_inc(s_root_out, 1)

            act.wait_ge(s_w_tr, 1)
            act.activation(W0.rearrange("p k f -> p (k f)"), banks[0][:, 0:2 * FEAT], ACT.Copy).then_inc(s_w_copied, 1)
            act.activation(W_src[:, 0:FEAT], banks[0][:, 2 * FEAT:3 * FEAT], ACT.Copy).then_inc(s_w_copied, 1)
            act.activation(W_res, banks[0][:, 3 * FEAT:4 * FEAT], ACT.Copy).then_inc(s_w_copied, 1)
            act.wait_ge(s_w_tr, 2)
            act.activation(W_src[:, FEAT:FEAT + SCORES], banks[1][:, 0:SCORES], ACT.Copy).then_inc(s_w_copied, 1)

            def feed(nl, sources, turn=True):
                n = len(sources)
                act.wait_ge(nl.start, 1)
                with act.Fori(0, TILES) as t:
                    if not turn:
                        act.wait_ge(nl.taken, t + 1)
                    for k, a in enumerate(sources):
                        act.activation(xs[:, k:k + 1, :], a[:, ds(t, 1), 0:FEAT], ACT.Copy).then_inc(nl.fetched, 1)
                    if turn:
                        act.wait_ge(nl.turned, t + 1)
                        act.activation(xT[:, 0:n, :], banks[0][:, 0:n * P].rearrange("p (k f) -> p k f", k=n),
                                       ACT.Copy).then_inc(nl.copied, 1)

            def copy_hotT(ps, scale=1.0, bias=0.0):
                def f(i, q):
                    act.wait_ge(ps.turned, when(i, q, 1 if ps is p1b else 5))
                    if ps is p1a:
                        act.wait_ge(ps.added, 16 * i + (4 * q + 12))
                    elif ps is p1b:
                        act.wait_ge(ps.spread, when(i, q, 1))
                    else:
                        act.wait_ge(ps.summed, when(i, q, 3))
                    act.activation(hotT[:, q % 2].rearrange("p u n -> p (u n)"), banks[4 + q % 2], ACT.Copy,
                                   scale=scale, bias=bias).then_inc(ps.hotT, 1)
                return f

            feed(n0, [X, acc])
            take_root(TILES)
            feed(n1a, [X])
            pipeline(act, [(copy_hotT(p1a, ABSENT, -ABSENT), 2)])
            act.wait_ge(s_self, 1)
            act.activation(selfw2, selfw, ACT.Exp).then_inc(s_selfexp, 1)

            def exponentials(i, q):
                act.wait_ge(p1b.used, when(i, q, 3))
                act.wait_ge(p1b.added, 16 * i + (4 * q + 4))
                act.activation(G[:, q, :, FEAT:ROW], e_arg[:, q % 2], ACT.Exp).then_inc(s_exp, 1)
            pipeline(act, [(copy_hotT(p1b), 2), (exponentials, 1)])
            feed(n1b, [X])
            take_root(FEAT)
            take_root(TILES)
            take_root(BUCKETS)

            def scale_hot(i, q):
                act.wait_ge(p2.hot, when(i, q, 1))
                for u in range(GROUP):
                    act.wait_ge(p2.used, 16 * i + (4 * q + u + 1))
                    for b in range(BASES):
                        ins = act.activation(wide[:, u, b, :], hot[:, q, u, :], ACT.Copy,
                                             scale=stS[:, q, u, 4 + b:5 + b])
                    ins.then_inc(p2.scaled, 1)
            pipeline(act, [(scale_hot, 0)])
            feed(n2, [rel_acc[:, :, b * P:(b + 1) * P] for b in range(BASES)], turn=False)
            take_root(TILES)
            feed(n3a, [X])

            def copy_recT(i, q):
                act.wait_ge(s_recT, when(i, q, 1))
                act.wait_ge(p3a.summed, when(i, q, 3))
                act.activation(recT[:, q % 2], banks[6 + q % 2][0:GROUP * SREC, 0:P],
                               ACT.Copy).then_inc(s_recTc, 1)

            def square(i, q):
                act.wait_ge(s_sqsum, when(i, q, 1))
                act.wait_ge(p3a.added, 16 * i + (4 * q + 4 + 16))
                act.activation(sq[:, q % 2], wide[:, q], ACT.Square).then_inc(s_square, 1)
                act.dma_start(hidden[:, ds(16 * i + 4 * q, 4), :], wide[:, q]).then_inc(s_hstored[q], 16)
            pipeline(act, [(copy_hotT(p3a), 2), (copy_recT, 1), (square, 0)])
            take_root(FEAT)

            def relu(i, q):
                act.wait_ge(p3b.scaled, when(i, q, 1))
                act.activation(wide[:, q], wide[:, q], ACT.Relu).then_inc(p3b.weighted, 1)
            pipeline(act, [(relu, 1)])
            feed(n3b, [acc])
            take_root(TILES)

        @block.tensor
        def _(pe):
            def load_tiles(row, i, q):
                _, v = nc.values_load_multi_w_load_instructions(
                    row[0:1, ds(16 * i + 4 * q, 4)], engines=[mybir.EngineType.PE], min_val=0,
                    max_val=BUCKETS - 1, skip_runtime_bounds_check_because="the maps hold tiles")
                return v

            for w in range(2):
                pe.wait_ge(s_prefix_in, w + 1)
                pe.matmul(banks[2][:, 0:BUCKETS], ones, cnt, start=True, stop=True)
                pe.matmul(banks[3][:, 0:BUCKETS], upper, cnt, start=True, stop=True).then_inc(s_prefix_out, 1)
            pe.wait_ge(s_prefix_in, 3)
            pe.matmul(banks[2][:, 0:2], ones, attr_sum, start=True, stop=True).then_inc(s_prefix_out, 1)
            pe.wait_ge(s_setup, 2)
            pe.wait_ge(s_wload, 16 * WLOADS)
            for k in range(4):
                ins = pe.transpose(banks[0][:, k * P:(k + 1) * P], raw[:, k, :], ident)
            ins.then_inc(s_w_tr, 1)
            pe.wait_ge(s_setup, 3)
            pe.matmul(banks[1][:, 0:SCORES], raw[:, 2, :], blockdiag, start=True, stop=True).then_inc(s_w_tr, 1)
            pe.wait_ge(s_maps, 32)
            pe.wait_ge(s_w_copied, 4)

            def scatter_hot(ps, width, ready=None):
                def f(i, q):
                    pe.wait_ge(ps.hot, when(i, q, 1))
                    pe.wait_ge(ps.added, 16 * i + (4 * q + 12))
                    if ready is None:
                        pe.wait_ge(s_gathered[q], ps.gathered(i))
                    else:
                        pe.wait_ge(ready, when(i, q, 1))
                    for u in range(GROUP):
                        rhs = wide[:, q, u, :] if ps is p3b else G[:, q, u, 0:width]
                        ins = pe.matmul(scatter_out(q, u, width), hot[:, q, u, :], rhs, start=True, stop=True)
                    ins.then_inc(ps.summed, 1)
                return f

            def turn_hot(ps):
                def f(i, q):
                    pe.wait_ge(ps.hot, when(i, q, 1))
                    pe.wait_ge(ps.hotT, when(i, q, 1))
                    for u in range(GROUP):
                        ins = pe.transpose(banks[4 + q % 2][:, u * P:(u + 1) * P], hot[:, q, u, :], ident)
                    ins.then_inc(ps.turned, 1)
                return f

            def count_src(i, q):
                pe.wait_ge(s_hotS, when(i, q, 1))
                pe.wait_ge(s_deg, 16 * i + (4 * q + 12))
                for u in range(GROUP):
                    ins = pe.matmul(banks[4 + q % 2][:, u:u + 1], wide[:, q, u, :], ones[:, 0:1], start=True, stop=True)
                ins.then_inc(p0.used, 1)

            pipeline(pe, [(count_src, 0), (scatter_hot(p0, FEAT + 1), 0)])

            def node_loop(nl, n, product, turn=True):
                with pe.Fori(0, TILES) as t:
                    pe.wait_ge(nl.fetched, n * t + n)
                    if turn:
                        for k in range(n):
                            ins = pe.transpose(banks[0][:, k * P:(k + 1) * P], xs[:, k, :], ident)
                        ins.then_inc(nl.turned, 1)
                        pe.wait_ge(nl.copied, t + 1)
                    pe.wait_ge(nl.taken, t + 1)
                    product().then_inc(nl.product, 1)

            def product0():
                pe.matmul(banks[1][:, 0:FEAT], xT[:, 0], W0[:, 0], start=True, stop=False)
                return pe.matmul(banks[1][:, 0:FEAT], xT[:, 1], W0[:, 1], start=False, stop=True)

            def product_of(weights, width):
                return lambda: pe.matmul(banks[1][:, 0:width], xT[:, 0], weights, start=True, stop=True)

            node_loop(n0, 2, product0)
            node_loop(n1a, 1, product_of(W_src, FEAT + SCORES))

            def spread_scores(i, q):
                pe.wait_ge(s_gathered[q], p1a.gathered(i))
                for u in range(GROUP):
                    pe.wait_ge(p1a.added, 16 * i + (4 * q + u + 13))
                    for h in range(HEADS):
                        ins = pe.matmul(banks[u][:, h * P:(h + 1) * P],
                                        G[:, q, u, h:h + 1].to_broadcast([P, P]), ident, start=True, stop=True)
                    ins.then_inc(p1a.spread, 1)
            pipeline(pe, [(turn_hot(p1a), 2), (spread_scores, 0)])

            def score_edges(i, q):
                pe.wait_ge(p1b.hotT, when(i, q, 3))
                pe.wait_ge(p1b.used, when(i, q, 1))
                tiles = load_tiles(mapD, i, q)
                for u in range(GROUP):
                    ins = pe.matmul(banks[6 + q % 2][:, 2 * HEADS * u:2 * HEADS * (u + 1)], hotT[:, q % 2, u, :],
                                    att[:, ds(tiles[u], 1), 0:2 * HEADS], start=True, stop=True)
                ins.then_inc(p1b.spread, 1)
            pe.wait_ge(s_selfexp, 2)
            pipeline(pe, [(turn_hot(p1b), 2), (score_edges, 1), (scatter_hot(p1b, ROW, p1b.weighted), 0)])
            node_loop(n1b, 1, product_of(W_res, FEAT))
            for k, a in enumerate((acc, squares)):
                pe.wait_ge(s_bn_in, k + 1)
                pe.matmul(banks[2][:, 0:FEAT], ones, a[:, 0, 0:FEAT], start=True, stop=False)
                with pe.Fori(1, TILES - 1) as t:
                    pe.matmul(banks[2][:, 0:FEAT], ones, a[:, ds(t, 1), 0:FEAT], start=False, stop=False)
                pe.matmul(banks[2][:, 0:FEAT], ones[0:LAST, :], a[0:LAST, TILES - 1, 0:FEAT],
                          start=False, stop=True).then_inc(s_bn_out, 1)
            def relation_sums(i, q):
                pe.wait_ge(s_gathered[q], p2.gathered(i))
                for u in range(GROUP):
                    pe.wait_ge(p2.scaled, 16 * i + (4 * q + u + 17))
                    pe.wait_ge(p2.added, 16 * i + (4 * q + u + 9))
                    pe.matmul(banks[4 * (q % 2) + u], G[:, q, u, 0:FEAT],
                              wide[:, u].rearrange("p b n -> p (b n)"), start=True, stop=True
                              ).then_inc(p2.used, 1)
            pipeline(pe, [(relation_sums, 0)])

            def product2():
                for b in range(BASES):
                    ins = pe.matmul(banks[1][:, 0:FEAT], xs[:, b, :], bases[:, b, :],
                                    start=(b == 0), stop=(b == BASES - 1))
                return ins
            node_loop(n2, BASES, product2, turn=False)
            node_loop(n3a, 1, product_of(W1.rearrange("p k f -> p (k f)"), 2 * FEAT))
            pe.wait_ge(s_mu_in, 1)
            pe.matmul(banks[2][:, 0:FEAT], ones, weighted_pq[:, 0, :], start=True, stop=False)
            with pe.Fori(1, TILES - 1) as t:
                pe.matmul(banks[2][:, 0:FEAT], ones, weighted_pq[:, ds(t, 1), :], start=False, stop=False)
            pe.matmul(banks[2][:, 0:FEAT], ones, weighted_pq[:, TILES - 1, :], start=False, stop=True
                      ).then_inc(s_mu, 1)

            def turn_records(i, q):
                pe.wait_ge(s_staged[q], p3a.staged(i))
                pe.wait_ge(s_recTc, when(i, q, 1))
                pe.transpose(banks[6 + q % 2][0:GROUP * SREC, 0:P],
                             stS[:, q].rearrange("p u k -> p (u k)"), ident).then_inc(s_recT, 1)

            def hidden_edges(i, q):
                pe.wait_ge(p3a.hotT, when(i, q, 3))
                pe.wait_ge(s_recTc, when(i, q, 3))
                pe.wait_ge(p3a.added, 16 * i + (4 * q + 12))
                tiles = load_tiles(mapS, i, q)
                for u in range(GROUP):
                    to = banks[q % 2][:, u * P:(u + 1) * P]
                    pe.matmul(to, hotT[:, q % 2, u, :], Pt[:, ds(tiles[u], 1), :], start=True, stop=False)
                    ins = pe.matmul(to, recT[:, q % 2], sel[:, u, :], start=False, stop=True)
                ins.then_inc(p3a.summed, 1)

            def sum_squares(i, q):
                pe.wait_ge(s_square, when(i, q, 5))
                pe.matmul(banks[3], ones, sq[:, q % 2].rearrange("p u n -> p (u n)"), start=False,
                          stop=False, skip_group_check=True).then_inc(s_sqsum, 1)
            pe.wait_ge(s_mu_in, 2)
            pe.matmul(banks[3], zeros, bases.rearrange("p b f -> p (b f)"), start=True, stop=False,
                      skip_group_check=True)
            pipeline(pe, [(turn_hot(p3a), 2), (turn_records, 2), (hidden_edges, 1), (sum_squares, 0)])
            pe.matmul(banks[3], zeros, bases.rearrange("p b f -> p (b f)"), start=False, stop=True,
                      skip_group_check=True).then_inc(s_mu, 1)
            pipeline(pe, [(scatter_hot(p3b, FEAT, p3b.weighted), 0)])
            node_loop(n3b, 1, product_of(W2, FEAT))

        @block.vector
        def _(dve):
            steps = [0]

            def then(ins):
                steps[0] += 1
                ins.then_inc(s_step, 1)
                dve.wait_ge(s_step, steps[0])

            def load_tiles(row, i, q):
                _, v = nc.values_load_multi_w_load_instructions(
                    row[0:1, ds(16 * i + 4 * q, 4)], engines=[mybir.EngineType.DVE], min_val=0,
                    max_val=BUCKETS - 1, skip_runtime_bounds_check_because="the maps hold tiles")
                return v

            for s, v in presets:
                dve.sem_inc(s, v)

            dve.memset(region[:, 0:5 * COLS], 0.0).then_inc(s_step, 1)
            dve.memset(zeros, 0.0).then_inc(s_step, 1)
            dve.memset(ones, 1.0).then_inc(s_step, 1)
            dve.memset(sel, 0.0).then_inc(s_step, 1)
            dve.memset(padS, 0.0).then_inc(s_step, 1)
            dve.memset(blockdiag, 0.0).then_inc(s_step, 1)
            dve.memset(att, 0.0).then_inc(s_step, 1)
            dve.memset(degs, 0.0).then_inc(s_step, 1)
            steps[0] = 8
            dve.wait_ge(s_step, steps[0])
            then(dve.memset(G[:, :, :, FEAT:FEAT + 1], 1.0))
            then(dve.memset(region[:, 0:2 * COLS].bitcast(I32), PAD_NODE))
            padS_v = padS.rearrange("p (c k) -> p c k", k=SREC)
            padD_v = padD.rearrange("p (c k) -> p c k", k=DREC)
            for v in (padS_v, padD_v):
                then(dve.memset(v[:, :, 0].bitcast(I32), PAD_NODE))
                then(dve.memset(v[:, :, 1], -1.0))
            dve.sem_inc(s_setup, 1)
            dve.wait_ge(s_const, 3)
            then(dve.tensor_scalar(ident, diff, 0.0, None, ALU.is_equal))
            then(dve.tensor_scalar(upper, diff, 0.0, None, ALU.is_gt))
            dve.sem_inc(s_setup, 1)

            def place_edges(w, key, rec, pos):
                as_int = mask.bitcast(I32)
                cum_i = cum.bitcast(I32)
                then(dve.tensor_scalar(as_int, key, TILE_SHIFT, None, ALU.logical_shift_right))
                then(dve.tensor_copy(tile_f, as_int))
                then(dve.tensor_scalar(as_int, key, P - 1, None, ALU.bitwise_and))
                then(dve.tensor_copy(rec[:, :, 1], as_int))
                with dve.Fori(0, BUCKETS) as t:
                    dve.wait_ge(s_cnt, t + (w * BUCKETS + 1))
                    dve.tensor_scalar(mask, tile_f, iota[:, ds(t, 1)], 0.0, ALU.is_equal, ALU.add,
                                      accum_out=cnt[:, ds(t, 1)]).then_inc(s_cnt, 1)
                dve.wait_ge(s_cnt, (w + 1) * BUCKETS + 1)
                dve.sem_inc(s_prefix_in, 1)
                dve.wait_ge(s_prefix_out, w + 1)
                then(dve.tensor_scalar(size, banks[2][:, 0:BUCKETS], float(P - 1), None, ALU.add))
                then(dve.tensor_copy(size_i, size))
                then(dve.tensor_scalar(size_i, size_i, TILE_SHIFT, None, ALU.logical_shift_right))
                then(dve.tensor_copy(size, size_i))
                then(dve.tensor_tensor_scan(ends, size, size, 0.0, ALU.add, ALU.max))
                then(dve.tensor_tensor(base, ends, size, ALU.subtract))
                then(dve.tensor_scalar(base, base, float(P), None, ALU.mult))
                then(dve.tensor_tensor(base, base, banks[3][:, 0:BUCKETS], ALU.add))
                shape = [P, MAPC, BUCKETS]
                then(dve.tensor_tensor(is_past, ends.unsqueeze(1).to_broadcast(shape),
                                       chunk_id.unsqueeze(2).to_broadcast(shape), ALU.is_le))
                then(dve.tensor_reduce(map_f, is_past, AX_X, ALU.add))
                then(dve.tensor_scalar(mapU[w], map_f, float(BUCKETS - 1), None, ALU.min))
                then(dve.memset(pos_f, 0.0))
                with dve.Fori(0, BUCKETS) as t:
                    k = t * 4 + w * 4 * BUCKETS
                    dve.tensor_scalar(mask, tile_f, iota[:, ds(t, 1)], None, ALU.is_equal).then_inc(s_rank, 1)
                    dve.wait_ge(s_rank, k + 1)
                    dve.tensor_tensor_scan(cum, mask, mask, base[:, ds(t, 1)], ALU.add, ALU.max).then_inc(s_rank, 1)
                    dve.wait_ge(s_rank, k + 2)
                    dve.tensor_tensor(cum, cum, mask, ALU.mult).then_inc(s_rank, 1)
                    dve.wait_ge(s_rank, k + 3)
                    dve.tensor_tensor(pos_f, pos_f, cum, ALU.add).then_inc(s_rank, 1)
                    dve.wait_ge(s_rank, k + 4)
                then(dve.tensor_scalar(pos_f, pos_f, -1.0, None, ALU.add))
                then(dve.tensor_copy(pos, pos_f))
                then(dve.tensor_scalar(as_int, pos, P - 1, None, ALU.bitwise_and))
                then(dve.tensor_scalar(cum_i, pos, TILE_SHIFT, None, ALU.logical_shift_right))
                then(dve.scalar_tensor_tensor(out=pos, in0=as_int, scalar=float(CHUNKS), in1=cum_i,
                                              op0=ALU.mult, op1=ALU.add))

            dve.sem_inc(s_cnt, 1)
            dve.wait_ge(s_keys, 96)
            then(dve.tensor_copy(natD[:, :, 0].bitcast(I32), key_s))
            place_edges(0, key_d, natD, pos_d)
            dve.sem_inc(s_nat[0], 1)
            then(dve.tensor_copy(natS[:, :, 0].bitcast(I32), key_d))
            place_edges(1, key_s, natS, pos_s)
            dve.wait_ge(s_kinds, 96)
            then(dve.tensor_copy(natS[:, :, 2:4], attr_in))
            then(dve.tensor_reduce(attr_sum, attr_in.rearrange("p c k -> p k c"), AX_X, ALU.add))
            dve.sem_inc(s_prefix_in, 1)
            dve.wait_ge(s_wload, 16 * WLOADS)
            then(dve.tensor_tensor(comps, comps, alpha.unsqueeze(2).to_broadcast([P, RELS, BASES]), ALU.mult))
            then(dve.tensor_copy(tile_f, kind))
            then(dve.memset(natS[:, :, 4:8], 0.0))
            comps_flat = comps.rearrange("p r b -> p (r b)")
            with dve.Fori(0, RELS) as r:
                dve.tensor_scalar(mask, tile_f, iota[:, ds(r, 1)], None, ALU.is_equal).then_inc(s_coef, 1)
                dve.wait_ge(s_coef, r * 5 + 1)
                for b in range(BASES):
                    c = natS[:, :, 4 + b]
                    dve.scalar_tensor_tensor(out=c, in0=mask, scalar=comps_flat[:, ds(r * BASES + b, 1)], in1=c,
                                             op0=ALU.mult, op1=ALU.add).then_inc(s_coef, 1)
                dve.wait_ge(s_coef, r * 5 + 5)
            dve.sem_inc(s_nat[1], 1)

            for j in range(SCORES):
                h = j % HEADS
                part = slice(CH * h, CH * (h + 1))
                dve.tensor_copy(blockdiag[part, j:j + 1], attcol[part, (0 if j < HEADS else 1):(1 if j < HEADS else 2)]
                                ).then_inc(s_step, 1)
            steps[0] += SCORES
            dve.wait_ge(s_step, steps[0])
            dve.sem_inc(s_setup, 1)
            dve.wait_ge(s_prefix_out, 3)
            then(dve.tensor_scalar(attr_mean, banks[2][:, 0:2], 1.0 / E, None, ALU.mult))

            for w in range(2):
                for q in range(RING):
                    dve.wait_ge(s_nscat[w][q], 64 * NAT_ROUNDS[q])
            then(dve.memset(acc_flat, 0.0))
            then(dve.memset(X[:, TILES - 1:BUCKETS, :], 0.0))
            dve.sem_inc(s_xpad, 1)
            dve.wait_ge(s_maps, 32)

            iota4 = iota.unsqueeze(1).to_broadcast([P, GROUP, P])

            def hot_of(ps, st, free, target=None, ready=None):
                def f(i, q):
                    free(i, q)
                    dve.wait_ge(s_staged[q], ps.staged(i))
                    dve.tensor_tensor((hot if target is None else target)[:, q], iota4,
                                      st[:, q, :, 1:2].to_broadcast([P, GROUP, P]), ALU.is_equal
                                      ).then_inc(ps.hot if ready is None else ready, 1)
                return f

            def free_when_summed(ps):
                return lambda i, q: dve.wait_ge(ps.summed, when(i, q, 1))

            def free_when_turned(ps):
                return lambda i, q: dve.wait_ge(ps.turned, when(i, q, 1))

            def add_sums(ps, row, width, also=None):
                def f(i, q):
                    tiles = load_tiles(row, i, q)
                    dve.wait_ge(ps.summed, when(i, q, 5))
                    for u in range(GROUP):
                        dve.wait_ge(ps.added, 16 * i + (4 * q + u + 16))
                        to = acc[:, ds(tiles[u], 1), 0:width]
                        dve.tensor_tensor(to, to, scatter_out(q, u, width).unsqueeze(1), ALU.add
                                          ).then_inc(ps.added, 1)
                return f

            def add_degrees(i, q):
                tiles = load_tiles(mapS, i, q)
                dve.wait_ge(p0.used, when(i, q, 5))
                for u in range(GROUP):
                    dve.wait_ge(s_deg, 16 * i + (4 * q + u + 16))
                    to = degs[:, ds(tiles[u], 1), 0:1]
                    dve.tensor_tensor(to, to, banks[4 + q % 2][:, u:u + 1].unsqueeze(1), ALU.add).then_inc(s_deg, 1)

            pipeline(dve, [(hot_of(p0, stS, lambda i, q: dve.wait_ge(p0.used, when(i, q, 1)), wide, s_hotS), 3),
                           (hot_of(p0, stD, free_when_summed(p0)), 3),
                           (add_degrees, 0), (add_sums(p0, mapD, FEAT + 1), 0)])
            dve.wait_ge(p0.added, 4 * GROUPS + 16)
            dve.wait_ge(s_deg, 4 * GROUPS + 16)

            def over_rows(column, tiles=TILES, width=FEAT):
                return column[:, 0:tiles].unsqueeze(2).to_broadcast([P, tiles, width])

            def over_nodes(row, tiles=TILES):
                return row.unsqueeze(1).to_broadcast([P, tiles, FEAT])

            Xt = X[:, 0:TILES, :]
            acc_t = acc[:, 0:TILES, 0:FEAT]
            roots = [0]

            def take_root():
                roots[0] += 1
                dve.sem_inc(s_root_in, 1)
                dve.wait_ge(s_root_out, roots[0])

            def layer_norm():
                then(dve.tensor_reduce(col[:, 0:TILES], Xt, AX_X, ALU.add))
                then(dve.tensor_scalar(col[:, 0:TILES], col[:, 0:TILES], 1.0 / FEAT, None, ALU.mult))
                then(dve.tensor_tensor(Xt, Xt, over_rows(col), ALU.subtract))
                then(dve.tensor_tensor(ln_tmp, Xt, Xt, ALU.mult))
                then(dve.tensor_reduce(col[:, 0:TILES], ln_tmp, AX_X, ALU.add))
                then(dve.tensor_scalar(root[:, 0:TILES], col[:, 0:TILES], 1.0 / FEAT, EPS, ALU.mult, ALU.add))
                take_root()
                then(dve.reciprocal(col[:, 0:TILES], root[:, 0:TILES]))
                then(dve.tensor_tensor(Xt, Xt, over_rows(col), ALU.mult))

            def node_loop(nl, take):
                dve.sem_inc(nl.start, 1)
                with dve.Fori(0, TILES) as t:
                    dve.wait_ge(nl.product, t + 1)
                    take(t)
                dve.wait_ge(nl.taken, TILES + 1)

            def add_to(target, nl):
                def take(t):
                    to = target[:, ds(t, 1), 0:FEAT]
                    dve.tensor_tensor(to, to, banks[1][:, 0:FEAT].unsqueeze(1), ALU.add).then_inc(nl.taken, 1)
                return take

            dve.wait_ge(s_x, 32)
            then(dve.tensor_copy(degs[:, :, 1], acc[:, :, FEAT]))
            then(dve.tensor_scalar(col, degs[:, :, 1], 1.0, None, ALU.max))
            then(dve.reciprocal(col2, col))
            then(dve.tensor_tensor(acc_t, acc_t, over_rows(col2), ALU.mult))
            node_loop(n0, add_to(X, n0))
            then(dve.tensor_tensor(Xt, Xt, over_nodes(rows["b0"]), ALU.add))
            layer_norm()

            then(dve.memset(acc_flat, 0.0))

            def take1(t):
                dve.tensor_copy(acc[:, ds(t, 1), 0:FEAT], banks[1][:, 0:FEAT].unsqueeze(1)).then_inc(n1a.taken2, 1)
                dve.tensor_copy(att[:, ds(t, 1), :], banks[1][:, FEAT:FEAT + SCORES].unsqueeze(1)
                                ).then_inc(n1a.taken2, 1)
                dve.wait_ge(n1a.taken2, 2 * t + 2)
                dve.sem_inc(n1a.taken, 1)
            node_loop(n1a, take1)
            dve.sem_inc(s_tables, 1)

            def take_max(i, q):
                tiles = load_tiles(mapD, i, q)
                dve.wait_ge(s_gathered[q], p1a.gathered(i))
                dve.wait_ge(p1a.hotT, when(i, q, 3))
                dve.tensor_copy(edge_score[:, ds(16 * i + 4 * q, 4), :], G[:, q, :, 0:HEADS]).then_inc(p1a.used, 1)
                for u in range(GROUP):
                    dve.wait_ge(p1a.spread, 16 * i + (4 * q + u + 1))
                    dve.wait_ge(p1a.added, 16 * i + (4 * q + u + 16))
                    dve.sem_inc(s_seen, 1)
                    for h in range(HEADS):
                        ins = dve.tensor_tensor_reduce(
                            out=wide[:, u, h, :], in0=banks[u][:, h * P:(h + 1) * P], in1=hotT[:, q % 2, u, :],
                            scale=1.0, scalar=-ABSENT, op0=ALU.add, op1=ALU.max,
                            accum_out=chunk_max[:, q % 2, u, h:h + 1])
                        ins.then_inc(p1a.weighted, 1)
                    dve.wait_ge(p1a.weighted, 64 * i + (16 * q + 4 * u + 4))
                    to = att[:, ds(tiles[u], 1), HEADS:2 * HEADS]
                    dve.tensor_tensor(to, to, chunk_max[:, q % 2, u:u + 1, :], ALU.max).then_inc(p1a.added, 1)
            pipeline(dve, [(hot_of(p1a, stD, free_when_turned(p1a)), 3), (take_max, 0)])
            dve.wait_ge(p1a.added, 4 * GROUPS + 16)
            dve.wait_ge(p1a.used, GROUPS)

            a_dst, a_max, a_src = (att[:, :, k * HEADS:(k + 1) * HEADS] for k in range(3))
            then(dve.tensor_tensor(selfw, a_dst, a_max, ALU.add))
            then(dve.scalar_tensor_tensor(out=a_max, in0=selfw, scalar=0.2, in1=selfw, op0=ALU.mult, op1=ALU.max))
            then(dve.tensor_tensor(selfw, a_dst, a_src, ALU.add))
            then(dve.scalar_tensor_tensor(out=selfw2, in0=selfw, scalar=0.2, in1=selfw, op0=ALU.mult, op1=ALU.max))
            then(dve.tensor_tensor(selfw, selfw2, a_max, ALU.subtract))
            dve.sem_inc(s_self, 1)
            dve.wait_ge(s_selfexp, 1)
            for h in range(HEADS):
                then(dve.tensor_tensor(acc[:, 0:TILES, h * CH:(h + 1) * CH], acc[:, 0:TILES, h * CH:(h + 1) * CH],
                                       selfw2[:, 0:TILES, h:h + 1].to_broadcast([P, TILES, CH]), ALU.mult))
            then(dve.tensor_copy(acc[:, :, FEAT:ROW], selfw2))
            dve.sem_inc(s_selfexp, 1)

            def edge_args(i, q):
                dve.wait_ge(p1b.spread, when(i, q, 3))
                dve.wait_ge(s_exp, when(i, q, 1))
                sc = banks[6 + q % 2][:, 0:GROUP * 2 * HEADS].rearrange("p (u k) -> p u k", u=GROUP)
                dve.tensor_tensor(e_sum[:, q % 2], edge_score[:, ds(16 * i + 4 * q, 4), :],
                                  sc[:, :, 0:HEADS], ALU.add).then_inc(p1b.scaled, 1)
                dve.wait_ge(p1b.scaled, 8 * i + (2 * q + 1))
                dve.scalar_tensor_tensor(out=e_lrelu[:, q % 2], in0=e_sum[:, q % 2], scalar=0.2,
                                         in1=e_sum[:, q % 2], op0=ALU.mult, op1=ALU.max).then_inc(p1b.scaled, 1)
                dve.wait_ge(p1b.scaled, 8 * i + (2 * q + 2))
                dve.tensor_tensor(e_arg[:, q % 2], e_lrelu[:, q % 2], sc[:, :, HEADS:2 * HEADS], ALU.subtract
                                  ).then_inc(p1b.used, 1)

            def weight_rows(i, q):
                dve.wait_ge(s_gathered[q], p1b.gathered(i))
                dve.wait_ge(s_exp, when(i, q, 3))
                r = G[:, q, :, 0:FEAT].rearrange("p u (h c) -> p u h c", h=HEADS)
                dve.tensor_tensor(r, r, G[:, q, :, FEAT:ROW].unsqueeze(3).to_broadcast([P, GROUP, HEADS, CH]),
                                  ALU.mult).then_inc(p1b.weighted, 1)
            pipeline(dve, [(hot_of(p1b, stD, free_when_summed(p1b)), 3), (edge_args, 1), (weight_rows, 0),
                           (add_sums(p1b, mapD, ROW), 0)])
            dve.wait_ge(p1b.added, 4 * GROUPS + 16)

            then(dve.tensor_scalar(selfw, acc[:, :, FEAT:ROW], 1e-16, None, ALU.add))
            then(dve.tensor_scalar(selfw[:, TILES:BUCKETS, :], selfw[:, TILES:BUCKETS, :], 1.0, None, ALU.max))
            then(dve.reciprocal(selfw2, selfw))
            for h in range(HEADS):
                then(dve.tensor_tensor(acc[:, 0:TILES, h * CH:(h + 1) * CH], acc[:, 0:TILES, h * CH:(h + 1) * CH],
                                       selfw2[:, 0:TILES, h:h + 1].to_broadcast([P, TILES, CH]), ALU.mult))
            node_loop(n1b, add_to(acc, n1b))
            then(dve.tensor_tensor(acc_t, acc_t, over_nodes(rows["bias1"]), ALU.add))
            dve.sem_inc(s_bn_in, 1)
            dve.wait_ge(s_bn_out, 1)
            then(dve.tensor_scalar(mean_row, banks[2][:, 0:FEAT], 1.0 / N, None, ALU.mult))
            then(dve.tensor_tensor(acc_t, acc_t, over_nodes(mean_row), ALU.subtract))
            then(dve.tensor_tensor(squares, acc_t, acc_t, ALU.mult))
            dve.sem_inc(s_bn_in, 1)
            dve.wait_ge(s_bn_out, 2)
            then(dve.tensor_scalar(root, banks[2][:, 0:FEAT], 1.0 / N, EPS, ALU.mult, ALU.add))
            take_root()
            then(dve.reciprocal(scale_row, root))
            then(dve.tensor_tensor(scale_row, scale_row, rows["gamma1"], ALU.mult))
            then(dve.tensor_tensor(acc_t, acc_t, over_nodes(scale_row), ALU.mult))
            then(dve.tensor_tensor(acc_t, acc_t, over_nodes(rows["beta1"]), ALU.add))
            then(dve.tensor_tensor(Xt, Xt, acc_t, ALU.add))
            layer_norm()

            then(dve.tensor_scalar(root[:, 0:BUCKETS], degs[:, :, 0], 1.0, None, ALU.max))
            take_root()
            then(dve.reciprocal(col, root[:, 0:BUCKETS]))
            then(dve.tensor_scalar(col2, degs[:, :, 0], 0.0, None, ALU.is_gt))
            then(dve.tensor_tensor(dinv, col, col2, ALU.mult))
            then(dve.tensor_tensor(ln_tmp, Xt, over_rows(dinv), ALU.mult))
            dve.sem_inc(s_tables, 1)
            dve.wait_ge(s_stored, 48)
            then(dve.memset(rel_flat, 0.0))

            def add_relations(i, q):
                tiles = load_tiles(mapS, i, q)
                for u in range(GROUP):
                    dve.wait_ge(p2.used, 16 * i + (4 * q + u + 5))
                    dve.wait_ge(p2.added, 16 * i + (4 * q + u + 16))
                    to = rel_acc[:, ds(tiles[u], 1), :]
                    dve.tensor_tensor(to, to, banks[4 * (q % 2) + u].unsqueeze(1), ALU.add).then_inc(p2.added, 1)
            pipeline(dve, [(hot_of(p2, stS, lambda i, q: dve.wait_ge(p2.scaled, 16 * i + (4 * q + 4))), 3),
                           (add_relations, 0)])
            dve.wait_ge(p2.added, 4 * GROUPS + 16)

            def take2(t):
                to = X[:, ds(t, 1), :]
                dve.scalar_tensor_tensor(out=to, in0=banks[1][:, 0:FEAT].unsqueeze(1), scalar=dinv[:, ds(t, 1)],
                                         in1=to, op0=ALU.mult, op1=ALU.add).then_inc(n2.taken, 1)
            node_loop(n2, take2)
            layer_norm()

            def take3(t):
                dve.tensor_copy(Pt[:, ds(t, 1), :], banks[1][:, 0:FEAT].unsqueeze(1)).then_inc(n3a.taken2, 1)
                dve.tensor_copy(acc[:, ds(t, 1), 0:FEAT], banks[1][:, FEAT:2 * FEAT].unsqueeze(1)
                                ).then_inc(n3a.taken2, 1)
                dve.wait_ge(n3a.taken2, 2 * t + 2)
                dve.sem_inc(n3a.taken, 1)
            node_loop(n3a, take3)
            dve.sem_inc(s_tables, 1)
            then(dve.tensor_tensor(weighted_pq, Pt[:, 0:TILES, :],
                                   degs[:, 0:TILES, 0:1].to_broadcast([P, TILES, FEAT]), ALU.mult))
            then(dve.tensor_tensor(weighted_q, acc_t, degs[:, 0:TILES, 1:2].to_broadcast([P, TILES, FEAT]), ALU.mult))
            then(dve.tensor_tensor(weighted_pq, weighted_pq, weighted_q, ALU.add))
            dve.sem_inc(s_mu_in, 1)
            dve.wait_ge(s_mu, 1)
            then(dve.tensor_scalar(mean_row, banks[2][:, 0:FEAT], 1.0 / E, None, ALU.mult))
            for k, n in enumerate(("w_attr0", "w_attr1")):
                then(dve.scalar_tensor_tensor(out=mean_row, in0=rows[n], scalar=attr_mean[:, k:k + 1],
                                              in1=mean_row, op0=ALU.mult, op1=ALU.add))
            then(dve.tensor_tensor(mean_row, mean_row, rows["b1"], ALU.add))
            then(dve.tensor_tensor(mean_row, rows["b1"], mean_row, ALU.subtract))
            then(dve.tensor_tensor(Pt[:, 0:TILES, :], Pt[:, 0:TILES, :], over_nodes(mean_row), ALU.add))
            then(dve.memset(Pt[:, TILES:BUCKETS, :], 0.0))
            dve.sem_inc(s_mu_in, 1)

            def make_hidden(i, q):
                dve.wait_ge(p3a.summed, when(i, q, 5))
                dve.wait_ge(s_gathered[q], p3a.gathered(i))
                dve.wait_ge(s_hstored[q], 16 * i + 16)
                dve.wait_ge(s_square, when(i, q, 1))
                dve.tensor_tensor(wide[:, q], banks[q % 2].rearrange("p (u n) -> p u n", u=GROUP),
                                  G[:, q, :, 0:FEAT], ALU.add).then_inc(p3a.added, 4)
            pipeline(dve, [(hot_of(p3a, stS, free_when_turned(p3a)), 3), (make_hidden, 0)])

            dve.wait_ge(s_mu, 2)
            then(dve.tensor_reduce(mean_row, banks[3].rearrange("p (u f) -> p f u", u=GROUP), AX_X, ALU.add))
            then(dve.tensor_scalar(root, mean_row, 1.0 / E, EPS, ALU.mult, ALU.add))
            take_root()
            then(dve.reciprocal(scale_row, root))
            then(dve.tensor_tensor(scale_row, scale_row, rows["gamma3"], ALU.mult))
            then(dve.memset(acc_flat, 0.0))

            def normalize(i, q):
                dve.wait_ge(s_hload[q], 16 * i + 16)
                dve.tensor_tensor(wide[:, q], wide[:, q], over_nodes(scale_row, GROUP), ALU.mult
                                  ).then_inc(p3b.used, 1)
                dve.wait_ge(p3b.used, when(i, q, 1))
                dve.tensor_tensor(wide[:, q], wide[:, q], over_nodes(rows["beta3"], GROUP), ALU.add
                                  ).then_inc(p3b.scaled, 1)
            pipeline(dve, [(hot_of(p3b, stS, free_when_summed(p3b)), 3), (normalize, 1),
                           (add_sums(p3b, mapS, FEAT), 0)])
            dve.wait_ge(p3b.added, 4 * GROUPS + 16)
            then(dve.tensor_scalar(col, degs[:, :, 0], 1.0, None, ALU.add))
            then(dve.reciprocal(col2, col))

            def take4(t):
                dve.scalar_tensor_tensor(out=mean_row, in0=rows["b2"], scalar=degs[:, ds(t, 1), 0],
                                         in1=banks[1][:, 0:FEAT], op0=ALU.mult, op1=ALU.add
                                         ).then_inc(n3b.taken2, 1)
                dve.wait_ge(n3b.taken2, 2 * t + 1)
                to = X[:, ds(t, 1), :]
                dve.scalar_tensor_tensor(out=scale_row.unsqueeze(1), in0=mean_row.unsqueeze(1),
                                         scalar=col2[:, ds(t, 1)], in1=to, op0=ALU.mult, op1=ALU.add
                                         ).then_inc(n3b.taken2, 1)
                dve.wait_ge(n3b.taken2, 2 * t + 2)
                dve.tensor_tensor(to, to, scale_row.unsqueeze(1), ALU.add).then_inc(n3b.taken, 1)
            node_loop(n3b, take4)
            layer_norm()
            dve.sem_inc(s_final, 1)


_INS = ["x", "src", "dst", "edge_attr_2", "edge_type_50", "L0_gnn_W", "L0_gnn_b", "L1_gnn_W_src",
        "L1_gnn_att_src", "L1_gnn_att_dst", "L1_gnn_W_res", "L1_gnn_bias", "L1_gnn_gamma", "L1_gnn_beta",
        "L2_gnn_bases", "L2_gnn_comps", "L2_gnn_alpha", "L3_gnn_W1", "L3_gnn_b1", "L3_gnn_gamma",
        "L3_gnn_beta", "L3_gnn_W2", "L3_gnn_b2"]


def kernel(**inputs):
    import numpy as _np
    import concourse.bacc as _bacc
    from concourse import mybir as _mybir
    from concourse.bass_utils import run_bass_kernel_spmd as _run

    nc = _bacc.Bacc("TRN2", target_bir_lowering=False, num_devices=1)
    arrays, args = {}, []
    for name in _INS:
        a = _np.ascontiguousarray(inputs[name])
        arrays[f"in_{name}_dram"] = a
        args.append(nc.dram_tensor(f"in_{name}_dram", a.shape, _mybir.dt.from_np(a.dtype), kind="ExternalInput").ap())
    out = nc.dram_tensor("out_0_dram", inputs["x"].shape, _mybir.dt.float32, kind="ExternalOutput").ap()
    gnn_program(nc, *args, out)
    r = _run(nc, [arrays], core_ids=[0])
    return r.results[0]["out_0_dram"]
```

```python
from contextlib import ExitStack

import concourse.bass as bass
from concourse import mybir

ALU = mybir.AluOpType
ACT = mybir.ActivationFunctionType
AX_X = mybir.AxisListType.X
F32 = mybir.dt.float32
I32 = mybir.dt.int32
U16 = mybir.dt.uint16
BF16 = mybir.dt.bfloat16
ds = bass.ds

P = 128
TILE_SHIFT = 7
PAIR_SHIFT = 8
FEAT = 128
HEADS = 4
CH = FEAT // HEADS
PAIR = 2
GROUP = 4
PAIRS_OF_GROUP = GROUP // PAIR
RING = 4
EPS = 1e-5
ABSENT = 1e30


def gnn_program(nc, x, src, dst, edge_attr, edge_type, L0_W, L0_b, L1_W_src, L1_att_src, L1_att_dst,
                L1_W_res, L1_bias, L1_gamma, L1_beta, L2_bases, L2_comps, L2_alpha, L3_W1, L3_b1,
                L3_gamma, L3_beta, L3_W2, L3_b2, out):
    N = x.shape[0]
    E = src.shape[0]
    TILES = -(-N // P)
    BUCKETS = TILES + 1
    LAST = N - (TILES - 1) * P
    COLS = -(-E // P)
    FULL = E // COLS
    REST = E - FULL * COLS
    PAD_NODE = TILES * P
    NODES = BUCKETS * P
    PAIR_EDGES = PAIR * P
    CHUNKS = (COLS * P + BUCKETS * (PAIR_EDGES - 1)) // PAIR_EDGES * PAIR
    CHUNKS = -(-CHUNKS // (GROUP * RING)) * GROUP * RING
    PAIRS = CHUNKS // PAIR
    MAPC = -(-PAIRS // P)
    GROUPS = CHUNKS // GROUP
    NAT_GROUPS = COLS // GROUP
    BLOCK = NAT_GROUPS // (4 * RING) * RING * GROUP
    BLOCKS = [(0, BLOCK), (BLOCK, 2 * BLOCK), (2 * BLOCK, 3 * BLOCK), (3 * BLOCK, COLS)]
    EARLY = 15 * RING * GROUP
    assert COLS % GROUP == 0 and FULL == P - 1
    RELS, BASES = L2_comps.shape
    DREC = 2
    SREC = 8
    ROW = FEAT + HEADS
    SCORES = 3 * HEADS

    def dram(name, shape, dt=F32):
        return nc.dram_tensor(name, shape, dt).ap()

    recD_dram = dram("rec_by_dst", (P * CHUNKS, DREC))
    recS_dram = dram("rec_by_src", (P * CHUNKS, SREC))
    mapD_dram = dram("tile_of_dst_pair", (P * MAPC,), U16)
    mapS_dram = dram("tile_of_src_pair", (P * MAPC,), U16)
    x_table = dram("x_table", (NODES, FEAT))
    xp_table = dram("xp_table", (NODES, ROW))
    xp_edges = dram("xp_edges", (P, CHUNKS, ROW))
    y_table = dram("y_table", (NODES, FEAT))
    q_table = dram("q_table", (NODES, FEAT))
    hidden = dram("hidden", (P, CHUNKS, FEAT))

    with ExitStack() as ctx:
        def sb(name, shape, dt=F32):
            return ctx.enter_context(nc.sbuf_tensor(name, shape, dt))[:]

        sem_names = []

        def sem(name):
            sem_names.append(name)
            return ctx.enter_context(nc.semaphore(name))

        NAT = 21 * COLS
        LAYERS = BUCKETS * FEAT * (1 + BASES)
        region = sb("region", [P, max(NAT, LAYERS)])
        nat = [region[:, n * COLS:(n + 1) * COLS] for n in range(21)]
        key_d, key_s, kind = (a.bitcast(I32) for a in nat[0:3])
        attr_in = region[:, 3 * COLS:5 * COLS].rearrange("p (c k) -> p c k", k=2)
        tile_f, mask, cum, pos_f = nat[5:9]
        pos_d, pos_s = nat[9].bitcast(I32), nat[12].bitcast(I32)
        natD = region[:, 10 * COLS:12 * COLS].rearrange("p (c k) -> p c k", k=DREC)
        src_tile = nat[11]
        natS = region[:, 13 * COLS:21 * COLS].rearrange("p (c k) -> p c k", k=SREC)
        at = BUCKETS * FEAT
        X = region[:, 0:at].rearrange("p (t f) -> p t f", f=FEAT)
        acc_flat = region[:, at:at + BUCKETS * ROW]
        acc = acc_flat.rearrange("p (t f) -> p t f", f=ROW)
        ln_tmp = region[:, at:at + TILES * FEAT].rearrange("p (t f) -> p t f", f=FEAT)
        rel_flat = region[:, at:at + BUCKETS * BASES * FEAT]
        rel_acc = rel_flat.rearrange("p (t f) -> p t f", f=BASES * FEAT)
        at += BUCKETS * ROW
        assert at + TILES * FEAT <= 12 * COLS
        squares = region[:, at:at + TILES * FEAT].rearrange("p (t f) -> p t f", f=FEAT)
        Pt_flat = region[:, at:at + BUCKETS * FEAT]
        Pt = Pt_flat.rearrange("p (t f) -> p t f", f=FEAT)
        at += BUCKETS * FEAT
        weighted_pq = region[:, at:at + TILES * FEAT].rearrange("p (t f) -> p t f", f=FEAT)

        at += TILES * FEAT
        weighted_q = region[:, at:at + TILES * FEAT].rearrange("p (t f) -> p t f", f=FEAT)

        G = sb("gathered", [P, RING, GROUP, ROW])
        hot = sb("hot", [P, RING, GROUP, P])
        hotT = sb("hotT", [P, 2, GROUP, P])
        wide = sb("wide", [P, RING, GROUP, P])
        sq = sb("sq", [P, 2, GROUP, P])
        stD = sb("staged_dst", [P, RING, GROUP, DREC])
        stS = sb("staged_src", [P, RING, GROUP, SREC])
        stP = sb("staged_pos", [P, RING, GROUP], I32)
        natS_ring = sb("nat_src_ring", [P, RING, GROUP, SREC])
        posS_ring = sb("pos_src_ring", [P, RING, GROUP], I32)
        mapD = sb("map_dst", [1, P * MAPC], U16)
        mapS = sb("map_src", [1, P * MAPC], U16)
        iota16 = sb("iota16", [P, P], BF16)
        ident16 = sb("ident16", [P, P], BF16)
        iota = sb("iota", [P, P])
        diff = sb("diff", [P, P])
        ident = sb("ident", [P, P])
        upper = sb("upper", [P, P])
        ones = sb("ones", [P, P])
        zeros = sb("zeros", [P, P])
        chunk_id = sb("chunk_id", [P, MAPC])
        cnt = sb("cnt", [P, BUCKETS])
        size = sb("size", [P, BUCKETS])
        size_i = sb("size_i", [P, BUCKETS], I32)
        ends = sb("ends", [P, BUCKETS])
        base = sb("base", [P, BUCKETS])
        is_past = sb("is_past", [P, MAPC, BUCKETS])
        map_f = sb("map_f", [P, MAPC])
        mapU = [sb("map_u_dst", [P, MAPC], U16), sb("map_u_src", [P, MAPC], U16)]
        comps = sb("comps", [P, RELS, BASES])
        alpha = sb("alpha", [P, RELS])
        attr_sum = sb("attr_sum", [P, 2])
        degs = sb("degs", [P, BUCKETS, 2])
        dinv = sb("dinv", [P, BUCKETS])
        col = sb("col", [P, BUCKETS])
        col2 = sb("col2", [P, BUCKETS])
        root = sb("root", [P, P])
        att = sb("att", [P, BUCKETS, SCORES])
        selfw = sb("selfw", [P, BUCKETS, HEADS])
        selfw2 = sb("selfw2", [P, BUCKETS, HEADS])
        chunk_max = sb("chunk_max", [P, 2, GROUP, HEADS])
        e_sum = sb("e_sum", [P, 2, GROUP, HEADS])
        e_lrelu = sb("e_lrelu", [P, 2, GROUP, HEADS])
        e_arg = sb("e_arg", [P, 2, GROUP, HEADS])
        raw = sb("raw", [P, 4, FEAT])
        blockdiag = sb("blockdiag", [P, SCORES])
        attcol = sb("attcol", [P, 2])
        W0 = sb("W0", [P, 2, FEAT])
        W_src = sb("W_src", [P, FEAT + SCORES])
        W_res = sb("W_res", [P, FEAT])
        bases = sb("bases", [P, BASES, FEAT])
        W1 = sb("W1", [P, 2, FEAT])
        W2 = sb("W2", [P, FEAT])
        row_names = ["b0", "bias1", "gamma1", "beta1", "b1", "w_attr0", "w_attr1", "gamma3", "beta3", "b2"]
        rows = {n: sb("row_" + n, [P, FEAT]) for n in row_names}
        mean_row = sb("mean_row", [P, FEAT])
        scale_row = sb("scale_row", [P, FEAT])
        attr_mean = sb("attr_mean", [P, 2])
        sel = sb("sel", [GROUP * SREC, GROUP, FEAT])
        recT = sb("recT", [GROUP * SREC, 2, P])
        xs = sb("tile_fetched", [P, 2, BASES, P])
        xT = sb("tile_turned", [P, 2, 2, P])
        hist = sb("hist", [P, P])

        banks = [ctx.enter_context(nc.psum_tensor(f"bank{i}", [P, 512], F32))[:] for i in range(8)]

        padD = hot.rearrange("p q u n -> p (q u n)")
        padS = hotT.rearrange("p q u n -> p (q u n)")
        PAD_D_COLS = RING * GROUP * P // DREC
        PAD_S_COLS = 2 * GROUP * P // SREC
        FILLS = -(-CHUNKS // PAD_D_COLS) + -(-CHUNKS // PAD_S_COLS)
        ROWS_LOADED = 10
        WLOADS = 10 + ROWS_LOADED + GROUP
        NAT_ROUNDS = [-(-(NAT_GROUPS - q) // RING) for q in range(RING)]

        hot16 = hot.rearrange("p q u n -> p (q u n)").bitcast(BF16)[:, 0:RING * GROUP * P].rearrange(
            "p (q u n) -> p q u n", q=RING, u=GROUP)
        tile16 = wide.rearrange("p q u n -> p (q u n)").bitcast(BF16)[:, 0:RING * GROUP * P].rearrange(
            "p (q u n) -> p q u n", q=RING, u=GROUP)
        place16 = hotT.rearrange("p q u n -> p (q u n)").bitcast(BF16)[:, 0:RING * GROUP * P].rearrange(
            "p (q u n) -> p q u n", q=RING, u=GROUP)
        turned16 = [banks[4 + k].bitcast(BF16)[:, 0:GROUP * P] for k in range(2)]

        def pair_out(q, j, width):
            return banks[q % 2][:, j * ROW:j * ROW + width]

        s_const = sem("const_ready")
        s_setup = sem("setup_steps")
        s_keys = sem("keys_loaded")
        s_kinds = sem("kinds_loaded")
        s_wload = sem("weights_loaded")
        s_x = sem("x_loaded")
        s_xpad = sem("x_pad_rows_zeroed")
        s_seen = sem("vector_seen")
        s_fill = sem("records_filled")
        s_table0 = sem("tables_zeroed")
        s_step = sem("vector_steps")
        s_cnt = sem("bucket_counts")
        s_rank = sem("rank_steps")
        s_coef = sem("coef_steps")
        s_prefix_in = sem("prefix_in")
        s_prefix_out = sem("prefix_out")
        s_nat = [sem("nat_by_dst_blocks"), sem("nat_by_src_ready")]
        s_mapped = sem("maps_stored")
        s_maps = sem("maps_loaded")
        s_nstage = [sem(f"nat_staged{q}") for q in range(RING)]
        s_ncopied = sem("nat_src_copied")
        s_hist_hot = sem("hist_hot")
        s_scale_row = sem("l3b_scale_row_ready")
        s_last_base = sem("l2_last_base_scaled")
        s_hist = sem("hist_summed")
        s_hist_out = sem("hist_out")
        s_nscat = [[sem(f"nat_scattered_{w}{q}") for q in range(RING)] for w in range(2)]
        s_go = sem("pool_go")
        s_root_in = sem("root_in")
        s_root_out = sem("root_out")
        s_w_tr = sem("weights_transposed")
        s_w_copied = sem("weights_copied")

        presets = []

        class Pass:

            def __init__(self, name, has, before, loads=1, gathers=True):
                def s(what):
                    return sem(f"{name}_{what}") if what in has.split() else None
                self.loads = loads
                self.staged0 = before.staged1 if before else 0
                self.gathered0 = before.gathered1 if before else 0
                self.staged1 = self.staged0 + 16 * loads * (GROUPS // RING)
                self.gathered1 = self.gathered0 + (16 * GROUPS if gathers else 0)
                self.hot = s("hot")
                self.turned = s("turned")
                self.hotT = s("hotT")
                self.spread = s("spread")
                self.used = s("used")
                self.weighted = s("weighted")
                self.scaled = s("scaled")
                self.summed = s("summed")
                self.added = sem(f"{name}_added") if name != "l1a" else None
                if self.added is not None:
                    presets.append((self.added, PAIRS_OF_GROUP * RING))

            def staged(self, i):
                return i * (16 * self.loads) + (16 * self.loads + self.staged0)

            def gathered(self, i):
                return i * (16 * GROUP) + (16 * GROUP + self.gathered0)

        class NodeLoop:

            def __init__(self, name):
                def s(what):
                    return sem(f"{name}_{what}")
                self.start = s("start")
                self.fetched = s("fetched")
                self.turned = s("turned")
                self.copied = s("copied")
                self.product = s("product")
                self.taken = s("taken")
                for one in (self.turned, self.copied, self.product, self.taken):
                    presets.append((one, 2))

        def when(i, q, more=0):
            return 4 * i + (q + more)

        def pipeline(eng, stages, groups=GROUPS, ring=RING):
            stages = [(*stage, groups)[:3] for stage in stages]
            ahead = max(lead for _, lead, _ in stages)
            last = (groups - ahead) // ring

            def step(i, q, within=groups):
                for f, lead, n in stages:
                    g = q + lead
                    if not isinstance(i, int):
                        if n >= within:
                            f(i + g // ring if g >= ring else i, g % ring)
                    elif 0 <= ring * i + g < n:
                        f((ring * i + g) // ring, g % ring)

            def loop(i0, i1, within):
                with eng.Fori(i0, i1) as i:
                    for q in range(ring):
                        step(i, q, within)

            for s in range(-ahead, ring):
                step(s // ring, s % ring)
            short = min(n for _, _, n in stages)
            if short < groups:
                until = min((n - lead) // ring for _, lead, n in stages if n == short)
                loop(1, until, short)
                for q in range(ring):
                    step(until, q)
                loop(until + 1, last, groups)
            else:
                loop(1, last, groups)
            for s in range(last * ring, groups):
                step(s // ring, s % ring)

        s_staged = [sem(f"records_staged{q}") for q in range(RING)]
        s_gathered = [sem(f"rows_gathered{q}") for q in range(RING)]
        p0 = Pass("l0", "hot summed", None)
        p1a = Pass("l1a", "hot turned hotT spread weighted", p0)
        p1b = Pass("l1b", "hot turned hotT spread used weighted scaled summed", p1a, loads=1, gathers=False)
        p2 = Pass("l2", "hot scaled used", p1b)
        p3a = Pass("l3a", "hot turned hotT summed", p2)
        p3b = Pass("l3b", "hot used scaled weighted summed", p3a, gathers=False)
        s_rows_stored = [sem(f"l1a_rows_stored{q}") for q in range(RING)]
        s_rows_loaded = [sem(f"l1b_rows_loaded{q}") for q in range(RING)]
        s_max = sem("l1a_max_taken")
        s_self = sem("l1_self_arg")
        s_selfexp = sem("l1_self_exp")
        s_exp = sem("l1b_exp")
        s_recT = sem("l3a_records_turned")
        s_recTc = sem("l3a_records_copied")
        s_square = sem("l3a_squares")
        s_sqsum = sem("l3a_squares_summed")
        s_hstored = [sem(f"l3a_hidden_stored{q}") for q in range(RING)]
        s_hload = [sem(f"l3b_hidden_loaded{q}") for q in range(RING)]
        for s in s_hstored + s_rows_stored:
            presets.append((s, 16))
        for ps in (p0, p1b, p3a, p3b):
            presets.append((ps.summed, RING))
        for ps in (p1a, p3a):
            presets.append((ps.turned, RING))
        for ps in (p1a, p1b, p3a):
            presets.append((ps.hotT, 2))
        presets += [(s_hist, RING), (p1a.weighted, 2 * PAIRS_OF_GROUP), (s_max, PAIRS_OF_GROUP * RING),
                    (p1b.spread, 2), (p1b.used, 2), (s_exp, 2), (s_last_base, RING),
                    (p2.used, 2 * GROUP), (p2.scaled, GROUP * RING), (s_recTc, 2), (s_square, RING), (s_sqsum, 2)]
        n0, n1a, n1b, n2, n3a, n3b = (NodeLoop(n) for n in ("n0", "n1a", "n1b", "n2", "n3a", "n3b"))
        s_bn_in = sem("bn_in")
        s_bn_out = sem("bn_out")
        s_tables = sem("tables_ready")
        s_stored = sem("tables_stored")
        s_mu_in = sem("mu_in")
        s_mu = sem("mu_out")
        s_last = sem("last_rows")
        s_final = sem("final_ready")
        s_out = sem("out_stored")

        def offset(ap):
            return bass.IndirectOffsetOnAxis(ap=ap, axis=0)

        block = ctx.enter_context(nc.Block())

        @block.sync
        def _(sp):
            def load_by_partition(flat, width, to, done):
                body = flat[0:FULL * COLS * width].rearrange("(p n) -> p n", p=FULL)
                most = FULL // 16 * 16
                sp.dma_start(to[0:most], body[0:most]).then_inc(done, 16)
                sp.dma_start(to[most:FULL], body[most:FULL]).then_inc(done, 16)
                sp.dma_start(to[FULL:FULL + 1, 0:REST * width],
                             flat[FULL * COLS * width:].rearrange("(p n) -> p n", p=1)).then_inc(done, 16)

            sp.wait_ge(s_setup, 1)
            load_by_partition(dst, 1, key_d, s_keys)
            load_by_partition(src, 1, key_s, s_keys)
            load_by_partition(edge_type, 1, kind, s_kinds)
            load_by_partition(edge_attr.rearrange("e k -> (e k)"), 2, region[:, 3 * COLS:5 * COLS], s_kinds)
            sp.dma_start(comps.rearrange("p r b -> p (r b)"),
                         L2_comps.rearrange("r b -> (r b)").partition_broadcast(P)).then_inc(s_wload, 16)
            sp.dma_start(alpha, L2_alpha.rearrange("r a -> (r a)").partition_broadcast(P)).then_inc(s_wload, 16)
            sp.dma_start(raw[:, 0:2, :], L0_W.rearrange("o (k f) -> o k f", k=2)).then_inc(s_wload, 16)
            sp.dma_start(raw[:, 2, :], L1_W_src).then_inc(s_wload, 16)
            sp.dma_start(raw[:, 3, :], L1_W_res).then_inc(s_wload, 16)
            with nc.allow_non_contiguous_dma(reason="one column of 128 values"):
                sp.dma_start(attcol[:, 0:1], L1_att_dst.rearrange("a h c -> (h c) a")).then_inc(s_wload, 16)
                sp.dma_start(attcol[:, 1:2], L1_att_src.rearrange("a h c -> (h c) a")).then_inc(s_wload, 16)
            sp.dma_start(bases, L2_bases.rearrange("b d f -> d b f")).then_inc(s_wload, 16)
            sp.dma_start(W1, L3_W1[0:2 * FEAT, :].rearrange("(k d) f -> d k f", k=2)).then_inc(s_wload, 16)
            sp.dma_start(W2, L3_W2).then_inc(s_wload, 16)
            row_src = {"b0": L0_b, "bias1": L1_bias, "gamma1": L1_gamma, "beta1": L1_beta, "b1": L3_b1,
                       "w_attr0": L3_W1[2 * FEAT, :], "w_attr1": L3_W1[2 * FEAT + 1, :],
                       "gamma3": L3_gamma, "beta3": L3_beta, "b2": L3_b2}
            for n in row_names:
                sp.dma_start(rows[n], row_src[n].partition_broadcast(P)).then_inc(s_wload, 16)
            for u in range(GROUP):
                r = u * SREC + 2
                sp.dma_start(sel[r:r + 2, u, :], L3_W1[2 * FEAT:2 * FEAT + 2, :]).then_inc(s_wload, 16)
            for c0 in range(0, CHUNKS, PAD_S_COLS):
                c1 = min(CHUNKS, c0 + PAD_S_COLS)
                sp.dma_start(recS_dram.rearrange("(p c) k -> p (c k)", p=P)[:, c0 * SREC:c1 * SREC],
                             padS[:, 0:(c1 - c0) * SREC]).then_inc(s_fill, 16)
            for c0 in range(0, CHUNKS, PAD_D_COLS):
                c1 = min(CHUNKS, c0 + PAD_D_COLS)
                sp.dma_start(recD_dram.rearrange("(p c) k -> p (c k)", p=P)[:, c0 * DREC:c1 * DREC],
                             padD[:, 0:(c1 - c0) * DREC]).then_inc(s_fill, 16)
            sp.dma_start(x_table[0:N, :], x).then_inc(s_table0, 16)
            sp.dma_start(x_table[N:PAD_NODE, :], zeros[0:PAD_NODE - N, :]).then_inc(s_table0, 16)
            for table in (x_table, y_table, q_table):
                sp.dma_start(table[PAD_NODE:NODES, :], zeros).then_inc(s_table0, 16)
            sp.dma_start(xp_table[PAD_NODE:NODES, 0:FEAT], zeros).then_inc(s_table0, 16)
            sp.dma_start(xp_table[PAD_NODE:NODES, FEAT:ROW], zeros[:, 0:HEADS]).then_inc(s_table0, 16)

            sp.wait_ge(s_fill, 16 * FILLS)

            def stage_nat(i, q, first=False):
                if not first:
                    sp.wait_ge(s_nscat[0][q], 64 * i)
                sp.dma_start(stD[:, q], natD[:, ds(16 * i + 4 * q, 4), :]).then_inc(s_nstage[q], 16)
                sp.dma_start(stP[:, q], pos_d[:, ds(16 * i + 4 * q, 4)]).then_inc(s_nstage[q], 16)

            for b, (c0, c1) in enumerate(BLOCKS):
                sp.wait_ge(s_nat[0], b + 1)
                g0, g1 = c0 // GROUP, c1 // GROUP
                if b == 0:
                    for q in range(RING):
                        stage_nat(0, q, first=True)
                with sp.Fori(g0 // RING + (b == 0), g1 // RING) as i:
                    for q in range(RING):
                        stage_nat(i, q)
            for q in range(NAT_GROUPS % RING):
                stage_nat(NAT_GROUPS // RING, q)

            sp.wait_ge(s_nat[1], 1)
            sp.dma_start(mapD_dram.rearrange("(p c) -> p c", p=P), mapU[0]).then_inc(s_mapped, 16)
            sp.dma_start(mapS_dram.rearrange("(p c) -> p c", p=P), mapU[1]).then_inc(s_mapped, 16)
            sp.wait_ge(s_mapped, 32)
            sp.dma_start(mapD, mapD_dram.rearrange("(a c) -> a c", a=1)).then_inc(s_maps, 16)
            sp.dma_start(mapS, mapS_dram.rearrange("(a c) -> a c", a=1)).then_inc(s_maps, 16)
            for q in range(RING):
                sp.wait_ge(s_nscat[0][q], 64 * NAT_ROUNDS[q])
            sp.dma_start(X[:, 0:TILES - 1, :], x[0:(TILES - 1) * P, :].rearrange("(t p) f -> p t f", p=P)).then_inc(s_x, 16)
            sp.wait_ge(s_xpad, 1)
            sp.dma_start(X[0:LAST, TILES - 1, :], x[(TILES - 1) * P:N, :]).then_inc(s_x, 16)
            sp.wait_ge(s_table0, 16 * 7)

            recD_view = recD_dram.rearrange("(p c) k -> p c k", p=P)
            recS_view = recS_dram.rearrange("(p c) k -> p c k", p=P)

            def stage_records(ps, st, view, also=None):
                def stage(i, q):
                    if not (isinstance(i, int) and i == 0):
                        if ps is p0:
                            sp.wait_ge(p0.summed, when(i, q, 1))
                        elif ps is p2:
                            sp.wait_ge(p2.used, 16 * i + (4 * q - 4))
                        elif ps is p3a:
                            sp.wait_ge(s_recT, when(i, q, -3))
                        else:
                            sp.wait_ge(ps.hot, when(i, q, -3))
                        if ps in (p1a, p2, p3a):
                            sp.wait_ge(s_gathered[q], i * (16 * GROUP) + ps.gathered0)
                    sp.dma_start(st[:, q], view[:, ds(16 * i + 4 * q, 4), :]).then_inc(s_staged[q], 16)
                pipeline(sp, [(stage, 0)] + ([(also, 0)] if also is not None else []))

            def load_rows(i, q):
                sp.wait_ge(p1b.summed, when(i, q, 1))
                sp.dma_start(G[:, q], xp_edges[:, ds(16 * i + 4 * q, 4), :]).then_inc(s_rows_loaded[q], 16)

            stage_records(p0, stD, recD_view)
            sp.wait_ge(s_tables, 1)
            table = xp_table[0:PAD_NODE, :].rearrange("(t p) f -> p t f", p=P)
            sp.dma_start(table[:, :, 0:FEAT], acc[:, 0:TILES, 0:FEAT]).then_inc(s_stored, 16)
            sp.dma_start(table[:, :, FEAT:ROW], att[:, 0:TILES, 2 * HEADS:SCORES]).then_inc(s_stored, 16)
            sp.wait_ge(s_stored, 32)
            stage_records(p1a, stD, recD_view)
            for q in range(RING):
                sp.wait_ge(s_rows_stored[q], 16 * (GROUPS // RING) + 16)
            sp.wait_ge(s_max, 2 * GROUPS + 8)
            for q in range(RING):
                sp.wait_ge(s_gathered[q], p1a.gathered1)
            stage_records(p1b, stD, recD_view, load_rows)
            sp.wait_ge(s_tables, 2)
            sp.dma_start(y_table[0:PAD_NODE, :].rearrange("(t p) f -> p t f", p=P), ln_tmp).then_inc(s_stored, 16)
            sp.wait_ge(s_stored, 48)
            for q in range(RING):
                sp.wait_ge(s_nscat[1][q], 64 * NAT_ROUNDS[q])
            stage_records(p2, stS, recS_view)
            sp.wait_ge(s_tables, 3)
            sp.dma_start(q_table[0:PAD_NODE, :].rearrange("(t p) f -> p t f", p=P),
                         acc[:, 0:TILES, 0:FEAT]).then_inc(s_stored, 16)
            sp.wait_ge(s_stored, 64)
            stage_records(p3a, stS, recS_view)
            sp.wait_ge(s_square, GROUPS + RING)
            for q in range(RING):
                sp.wait_ge(s_hstored[q], 16 * (GROUPS // RING) + 16)

            def load_hidden(i, q):
                sp.wait_ge(p3b.summed, when(i, q, 1))
                sp.dma_start(wide[:, q], hidden[:, ds(16 * i + 4 * q, 4), :]).then_inc(s_hload[q], 16)
            stage_records(p3b, stS, recS_view, load_hidden)
            sp.wait_ge(s_final, 1)
            sp.dma_start(out[0:(TILES - 1) * P, :].rearrange("(t p) f -> p t f", p=P), X[:, 0:TILES - 1, :]).then_inc(s_out, 16)
            sp.dma_start(out[(TILES - 1) * P:N, :], X[0:LAST, TILES - 1, :]).then_inc(s_out, 16)
            sp.wait_ge(s_out, 32)

        @block.gpsimd
        def _(pool):
            pool.iota(iota, [[1, P]], base=0, channel_multiplier=0,
                      allow_small_or_imprecise_dtypes=True).then_inc(s_const, 1)
            pool.iota(diff, [[1, P]], base=0, channel_multiplier=-1,
                      allow_small_or_imprecise_dtypes=True).then_inc(s_const, 1)
            pool.iota(chunk_id, [[1, MAPC]], base=0, channel_multiplier=MAPC,
                      allow_small_or_imprecise_dtypes=True).then_inc(s_const, 1)

            def scatter_dst(i, q):
                pool.wait_ge(s_nstage[q], 32 * i + 32)
                pool.sem_inc(s_go, 1)
                for u in range(GROUP):
                    pool.indirect_dma_start(out=recD_dram, out_offset=offset(stP[:, q, u:u + 1]),
                                            in_=stD[:, q, u, :], in_offset=None).then_inc(s_nscat[0][q], 16)
            with pool.Fori(0, NAT_GROUPS // RING) as i:
                for q in range(RING):
                    scatter_dst(i, q)
            for q in range(NAT_GROUPS % RING):
                scatter_dst(NAT_GROUPS // RING, q)

            def scatter_src(i, q, first=False):
                if not first:
                    pool.wait_ge(s_nscat[1][q], 64 * i)
                    pool.sem_inc(s_go, 1)
                pool.tensor_copy(natS_ring[:, q], natS[:, ds(16 * i + 4 * q, 4), :]).then_inc(s_ncopied, 1)
                pool.tensor_copy(posS_ring[:, q], pos_s[:, ds(16 * i + 4 * q, 4)]).then_inc(s_ncopied, 1)
                pool.wait_ge(s_ncopied, 8 * i + (2 * q + 2))
                pool.sem_inc(s_go, 1)
                for u in range(GROUP):
                    pool.indirect_dma_start(out=recS_dram, out_offset=offset(posS_ring[:, q, u:u + 1]),
                                            in_=natS_ring[:, q, u, :], in_offset=None).then_inc(s_nscat[1][q], 16)

            def gather_rows(ps, st, table, width):
                def gather(i, q):
                    if ps is p1a:
                        pool.wait_ge(s_rows_stored[q], 16 * i + 16)
                        if not (isinstance(i, int) and i == 0):
                            pool.wait_ge(p1a.spread, 8 * i + (2 * q - 6))
                    elif ps is p0:
                        pool.wait_ge(p0.summed, when(i, q, 1))
                    elif ps is p2:
                        if not (isinstance(i, int) and i == 0):
                            pool.wait_ge(p2.used, 16 * i + (4 * q - 4))
                    else:
                        pool.wait_ge(p3a.added, 8 * i + (2 * q + 2))
                    pool.wait_ge(s_staged[q], ps.staged(i))
                    pool.sem_inc(s_go, 1)
                    for u in range(GROUP):
                        pool.indirect_dma_start(out=G[:, q, u, 0:width], out_offset=None, in_=table,
                                                in_offset=offset(st[:, q, u, 0:1].bitcast(I32))
                                                ).then_inc(s_gathered[q], 16)
                for q in range(RING):
                    gather(0, q)
                with pool.Fori(1, GROUPS // RING) as i:
                    for q in range(RING):
                        gather(i, q)

            gather_rows(p0, stD, x_table, FEAT)
            pool.wait_ge(s_nat[1], 1)
            for q in range(RING):
                scatter_src(0, q, first=True)
            with pool.Fori(1, EARLY // (RING * GROUP)) as i:
                for q in range(RING):
                    scatter_src(i, q)
            gather_rows(p1a, stD, xp_table, ROW)
            with pool.Fori(EARLY // (RING * GROUP), NAT_GROUPS // RING) as i:
                for q in range(RING):
                    scatter_src(i, q)
            for q in range(NAT_GROUPS % RING):
                scatter_src(NAT_GROUPS // RING, q)
            gather_rows(p2, stS, y_table, FEAT)
            gather_rows(p3a, stS, q_table, FEAT)

            def scale_hidden(i, q):
                pool.wait_ge(s_hload[q], 16 * i + 16)
                pool.tensor_tensor(wide[:, q], wide[:, q], scale_row.unsqueeze(1).to_broadcast([P, GROUP, FEAT]),
                                   ALU.mult).then_inc(p3b.used, 1)
            pool.wait_ge(s_scale_row, 1)
            pipeline(pool, [(scale_hidden, 0)])

        @block.scalar
        def _(act):
            roots = [0]

            def take_root(width):
                roots[0] += 1
                act.wait_ge(s_root_in, roots[0])
                act.activation(root[:, 0:width], root[:, 0:width], ACT.Sqrt).then_inc(s_root_out, 1)

            act.wait_ge(s_w_tr, 1)
            act.activation(W0.rearrange("p k f -> p (k f)"), banks[0][:, 0:2 * FEAT], ACT.Copy).then_inc(s_w_copied, 1)
            act.activation(W_src[:, 0:FEAT], banks[0][:, 2 * FEAT:3 * FEAT], ACT.Copy).then_inc(s_w_copied, 1)
            act.activation(W_res, banks[0][:, 3 * FEAT:4 * FEAT], ACT.Copy).then_inc(s_w_copied, 1)
            act.wait_ge(s_w_tr, 2)
            act.activation(W_src[:, FEAT:FEAT + SCORES], banks[1][:, 0:SCORES], ACT.Copy).then_inc(s_w_copied, 1)

            def feed(nl, sources, turn=True):
                n = len(sources)

                def fetch(t2, r):
                    act.wait_ge(nl.turned if turn else nl.product, t2 * 2 + (r + 1))
                    for k, a in enumerate(sources):
                        act.activation(xs[:, r, k:k + 1, :], a[:, ds(t2 * 2 + r, 1), 0:FEAT], ACT.Copy
                                       ).then_inc(nl.fetched, 1)

                def bring_back(t2, r):
                    act.wait_ge(nl.turned, t2 * 2 + (r + 3))
                    act.wait_ge(nl.product, t2 * 2 + (r + 1))
                    act.activation(xT[:, r, 0:n, :], banks[r][:, 0:n * P].rearrange("p (k f) -> p k f", k=n),
                                   ACT.Copy).then_inc(nl.copied, 1)
                act.wait_ge(nl.start, 1)
                pipeline(act, [(fetch, 1)] + ([(bring_back, 0)] if turn else []), groups=TILES, ring=2)

            def copy_hotT(ps, scale=1.0, bias=0.0):
                def f(i, q):
                    act.wait_ge(ps.turned, when(i, q, 1 if ps is p1b else 5))
                    if ps is p1a:
                        act.wait_ge(p1a.weighted, 8 * i + (2 * q + 2))
                    elif ps is p1b:
                        act.wait_ge(ps.spread, when(i, q, 1))
                    else:
                        act.wait_ge(ps.summed, when(i, q, 3))
                    act.activation(hotT[:, q % 2].rearrange("p u n -> p (u n)"),
                                   turned16[q % 2] if ps is p1a else banks[4 + q % 2], ACT.Copy,
                                   scale=scale, bias=bias).then_inc(ps.hotT, 1)
                return f

            act.wait_ge(s_hist_out, 1)
            act.activation(hist, banks[7][:, 0:P], ACT.Copy).then_inc(s_hist_out, 1)
            feed(n0, [X, acc])
            take_root(TILES)
            feed(n1a, [X])

            def store_rows(i, q):
                act.wait_ge(s_gathered[q], p1a.gathered(i))
                act.dma_start(xp_edges[:, ds(16 * i + 4 * q, 4), :], G[:, q]).then_inc(s_rows_stored[q], 16)
            pipeline(act, [(store_rows, 1), (copy_hotT(p1a, ABSENT, -ABSENT), 2)])
            act.wait_ge(s_self, 1)
            act.activation(selfw2, selfw, ACT.Exp).then_inc(s_selfexp, 1)

            def exponentials(i, q):
                act.wait_ge(p1b.used, when(i, q, 3))
                act.wait_ge(s_rows_loaded[q], 16 * i + 16)
                act.activation(G[:, q, :, FEAT:ROW], e_arg[:, q % 2], ACT.Exp).then_inc(s_exp, 1)
            pipeline(act, [(copy_hotT(p1b), 3), (exponentials, 2)])
            feed(n1b, [X])
            take_root(FEAT)
            take_root(TILES)
            take_root(BUCKETS)

            def scale_hot(i, q):
                act.wait_ge(p2.hot, when(i, q, 1))
                for u in range(GROUP):
                    act.wait_ge(p2.used, 16 * i + (4 * q + u + 5))
                    for b in range(BASES - 1):
                        ins = act.activation(wide[:, u, b, :], hot[:, q, u, :], ACT.Copy,
                                             scale=stS[:, q, u, 4 + b:5 + b])
                    ins.then_inc(p2.scaled, 1)
            pipeline(act, [(scale_hot, 0)])
            feed(n2, [rel_acc[:, :, b * P:(b + 1) * P] for b in range(BASES)], turn=False)
            take_root(TILES)
            feed(n3a, [X])

            def copy_recT(i, q):
                act.wait_ge(s_recT, when(i, q, 1))
                act.wait_ge(p3a.summed, when(i, q, 3))
                act.activation(recT[:, q % 2], banks[6 + q % 2][0:GROUP * SREC, 0:P],
                               ACT.Copy).then_inc(s_recTc, 1)

            def square(i, q):
                act.wait_ge(s_sqsum, when(i, q, 1))
                act.wait_ge(p3a.added, 8 * i + (2 * q + 10))
                act.activation(sq[:, q % 2], wide[:, q], ACT.Square).then_inc(s_square, 1)
                act.dma_start(hidden[:, ds(16 * i + 4 * q, 4), :], wide[:, q]).then_inc(s_hstored[q], 16)
            pipeline(act, [(copy_hotT(p3a), 2), (copy_recT, 2), (square, 0)])
            take_root(FEAT)

            def relu(i, q):
                act.wait_ge(p3b.scaled, when(i, q, 1))
                act.activation(wide[:, q], wide[:, q], ACT.Relu).then_inc(p3b.weighted, 1)
            pipeline(act, [(relu, 1)])
            feed(n3b, [acc])
            take_root(TILES)

        @block.tensor
        def _(pe):
            def load_tiles(row, i, q):
                _, v = nc.values_load_multi_w_load_instructions(
                    row[0:1, ds(8 * i + 2 * q, 2)], engines=[mybir.EngineType.PE], min_val=0,
                    max_val=BUCKETS - 1, skip_runtime_bounds_check_because="the maps hold tiles")
                return v

            for w in range(2):
                pe.wait_ge(s_prefix_in, w + 1)
                pe.matmul(banks[2][:, 0:BUCKETS], ones, cnt, start=True, stop=True)
                pe.matmul(banks[3][:, 0:BUCKETS], upper, cnt, start=True, stop=True).then_inc(s_prefix_out, 1)
            pe.wait_ge(s_prefix_in, 3)
            pe.matmul(banks[2][:, 0:2], ones, attr_sum, start=True, stop=True).then_inc(s_prefix_out, 1)
            pe.wait_ge(s_setup, 2)
            pe.wait_ge(s_wload, 16 * WLOADS)
            for k in range(4):
                ins = pe.transpose(banks[0][:, k * P:(k + 1) * P], raw[:, k, :], ident)
            ins.then_inc(s_w_tr, 1)
            pe.wait_ge(s_setup, 3)
            pe.matmul(banks[1][:, 0:SCORES], raw[:, 2, :], blockdiag, start=True, stop=True).then_inc(s_w_tr, 1)
            pe.wait_ge(s_maps, 32)
            pe.wait_ge(s_w_copied, 4)

            def scatter_hot(ps, width, ready=None):
                def f(i, q):
                    pe.wait_ge(ps.hot, when(i, q, 1))
                    pe.wait_ge(ps.added, 8 * i + (2 * q + 6))
                    if ready is None:
                        pe.wait_ge(s_gathered[q], ps.gathered(i))
                    else:
                        pe.wait_ge(ready, when(i, q, 1))
                    for u in range(GROUP):
                        rhs = wide[:, q, u, :] if ps is p3b else G[:, q, u, 0:width]
                        ins = pe.matmul(pair_out(q, u // PAIR, width), hot[:, q, u, :], rhs,
                                        start=(u % PAIR == 0), stop=(u % PAIR == PAIR - 1))
                    ins.then_inc(ps.summed, 1)
                return f

            def turn_hot(ps):
                def f(i, q):
                    pe.wait_ge(ps.hot, when(i, q, 1))
                    pe.wait_ge(ps.hotT, when(i, q, 1))
                    for u in range(GROUP):
                        if ps is p1a:
                            ins = pe.transpose(turned16[q % 2][:, u * P:(u + 1) * P], hot16[:, q, u, :], ident16)
                        else:
                            ins = pe.transpose(banks[4 + q % 2][:, u * P:(u + 1) * P], hot[:, q, u, :], ident)
                    ins.then_inc(ps.turned, 1)
                return f

            def histogram(i, q):
                pe.wait_ge(s_hist_hot, 8 * i + (2 * q + 2))
                for u in range(GROUP):
                    ins = pe.matmul(banks[7][0:BUCKETS, 0:P], tile16[:, q, u, 0:BUCKETS], place16[:, q, u, :],
                                    start=False, stop=False, skip_group_check=True)
                ins.then_inc(s_hist, 1)
            pe.matmul(banks[7][:, 0:P], zeros, zeros, start=True, stop=False, skip_group_check=True)
            pipeline(pe, [(scatter_hot(p0, FEAT + 1), 0), (histogram, 0, NAT_GROUPS)])
            pe.matmul(banks[7][:, 0:P], zeros, zeros, start=False, stop=True, skip_group_check=True
                      ).then_inc(s_hist_out, 1)
            pe.wait_ge(s_hist_out, 2)
            pe.transpose(banks[6][:, 0:P], hist, ident).then_inc(s_hist_out, 1)

            def node_loop(nl, n, product, turn=True):
                def turn_tile(t2, r):
                    pe.wait_ge(nl.fetched, t2 * (2 * n) + (n * r + n))
                    pe.wait_ge(nl.copied, t2 * 2 + (r + 1))
                    for k in range(n):
                        ins = pe.transpose(banks[r][:, k * P:(k + 1) * P], xs[:, r, k, :], ident)
                    ins.then_inc(nl.turned, 1)

                def multiply(t2, r):
                    if turn:
                        pe.wait_ge(nl.copied, t2 * 2 + (r + 3))
                    else:
                        pe.wait_ge(nl.fetched, t2 * (2 * n) + (n * r + n))
                    pe.wait_ge(nl.taken, t2 * 2 + (r + 1))
                    product(banks[2 + r], r).then_inc(nl.product, 1)
                pipeline(pe, ([(turn_tile, 1)] if turn else []) + [(multiply, 0)], groups=TILES, ring=2)

            def product0(to, r):
                pe.matmul(to[:, 0:FEAT], xT[:, r, 0], W0[:, 0], start=True, stop=False)
                return pe.matmul(to[:, 0:FEAT], xT[:, r, 1], W0[:, 1], start=False, stop=True)

            def product_of(weights, width):
                return lambda to, r: pe.matmul(to[:, 0:width], xT[:, r, 0], weights, start=True, stop=True)

            node_loop(n0, 2, product0)
            node_loop(n1a, 1, product_of(W_src, FEAT + SCORES))

            def spread_scores(i, q):
                pe.wait_ge(s_gathered[q], p1a.gathered(i))
                for j in range(PAIRS_OF_GROUP):
                    pe.wait_ge(p1a.weighted, 8 * i + (2 * q + j + 3))
                    for h in range(HEADS):
                        for c in range(PAIR):
                            at_ = (h % 2) * PAIR_EDGES + c * P
                            score = G[:, q, PAIR * j + c, FEAT + h:FEAT + h + 1]
                            ins = pe.matmul(banks[2 * j + h // 2][:, at_:at_ + P], score.to_broadcast([P, P]),
                                            ident, start=True, stop=True)
                    ins.then_inc(p1a.spread, 1)
            pipeline(pe, [(turn_hot(p1a), 2), (spread_scores, 0)])

            def score_edges(i, q):
                pe.wait_ge(p1b.hotT, when(i, q, 3))
                pe.wait_ge(p1b.used, when(i, q, 1))
                tiles = load_tiles(mapD, i, q)
                for u in range(GROUP):
                    ins = pe.matmul(banks[6 + q % 2][:, 2 * HEADS * u:2 * HEADS * (u + 1)], hotT[:, q % 2, u, :],
                                    att[:, ds(tiles[u // PAIR], 1), 0:2 * HEADS], start=True, stop=True)
                ins.then_inc(p1b.spread, 1)
            pe.wait_ge(s_selfexp, 2)
            pipeline(pe, [(score_edges, 2), (turn_hot(p1b), 3), (scatter_hot(p1b, ROW, p1b.weighted), 1)])
            node_loop(n1b, 1, product_of(W_res, FEAT))
            for k, a in enumerate((acc, squares)):
                pe.wait_ge(s_bn_in, k + 1)
                pe.matmul(banks[4][:, 0:FEAT], ones, a[:, 0, 0:FEAT], start=True, stop=False)
                with pe.Fori(1, TILES - 1) as t:
                    pe.matmul(banks[4][:, 0:FEAT], ones, a[:, ds(t, 1), 0:FEAT], start=False, stop=False)
                pe.matmul(banks[4][:, 0:FEAT], ones[0:LAST, :], a[0:LAST, TILES - 1, 0:FEAT],
                          start=False, stop=True).then_inc(s_bn_out, 1)
            def relation_sums(i, q):
                pe.wait_ge(s_gathered[q], p2.gathered(i))
                pe.wait_ge(s_last_base, when(i, q, 5))
                wide_bases = (BASES - 1) * P
                for u in range(GROUP):
                    first, final = u % PAIR == 0, u % PAIR == PAIR - 1
                    to = banks[2 * (q % 2) + u // PAIR]
                    pe.wait_ge(p2.scaled, 16 * i + (4 * q + u + 17))
                    if first:
                        pe.wait_ge(p2.added, 8 * i + (2 * q + u // PAIR + 5))
                    ins = pe.matmul(to[:, 0:wide_bases], G[:, q, u, 0:FEAT],
                                    wide[:, u, 0:BASES - 1].rearrange("p b n -> p (b n)"), start=first, stop=final)
                    if final:
                        for v in range(u - PAIR + 1, u + 1):
                            ins = pe.matmul(to[:, wide_bases:], G[:, q, v, 0:FEAT], sq[:, q % 2, v, :],
                                            start=(v == u - PAIR + 1), stop=(v == u))
                    ins.then_inc(p2.used, 1)
            pipeline(pe, [(relation_sums, 0)])

            def product2(to, r):
                for b in range(BASES):
                    ins = pe.matmul(to[:, 0:FEAT], xs[:, r, b, :], bases[:, b, :],
                                    start=(b == 0), stop=(b == BASES - 1))
                return ins
            node_loop(n2, BASES, product2, turn=False)
            node_loop(n3a, 1, product_of(W1.rearrange("p k f -> p (k f)"), 2 * FEAT))
            pe.wait_ge(s_mu_in, 1)
            pe.matmul(banks[4][:, 0:FEAT], ones, weighted_pq[:, 0, :], start=True, stop=False)
            with pe.Fori(1, TILES - 1) as t:
                pe.matmul(banks[4][:, 0:FEAT], ones, weighted_pq[:, ds(t, 1), :], start=False, stop=False)
            pe.matmul(banks[4][:, 0:FEAT], ones, weighted_pq[:, TILES - 1, :], start=False, stop=True
                      ).then_inc(s_mu, 1)

            def turn_records(i, q):
                pe.wait_ge(s_staged[q], p3a.staged(i))
                pe.wait_ge(s_recTc, when(i, q, 1))
                pe.transpose(banks[6 + q % 2][0:GROUP * SREC, 0:P],
                             stS[:, q].rearrange("p u k -> p (u k)"), ident).then_inc(s_recT, 1)

            def hidden_edges(i, q):
                pe.wait_ge(p3a.hotT, when(i, q, 3))
                pe.wait_ge(s_recTc, when(i, q, 3))
                pe.wait_ge(p3a.added, 8 * i + (2 * q + 6))
                tiles = load_tiles(mapS, i, q)
                for u in range(GROUP):
                    to = banks[q % 2][:, u * P:(u + 1) * P]
                    pe.matmul(to, hotT[:, q % 2, u, :], Pt[:, ds(tiles[u // PAIR], 1), :], start=True, stop=False)
                    ins = pe.matmul(to, recT[:, q % 2], sel[:, u, :], start=False, stop=True)
                ins.then_inc(p3a.summed, 1)

            def sum_squares(i, q):
                pe.wait_ge(s_square, when(i, q, 5))
                pe.matmul(banks[3], ones, sq[:, q % 2].rearrange("p u n -> p (u n)"), start=False,
                          stop=False, skip_group_check=True).then_inc(s_sqsum, 1)
            pe.wait_ge(s_mu_in, 2)
            pe.matmul(banks[3], zeros, bases.rearrange("p b f -> p (b f)"), start=True, stop=False,
                      skip_group_check=True)
            pipeline(pe, [(hidden_edges, 1), (turn_hot(p3a), 2), (turn_records, 2), (sum_squares, 0)])
            pe.matmul(banks[3], zeros, bases.rearrange("p b f -> p (b f)"), start=False, stop=True,
                      skip_group_check=True).then_inc(s_mu, 1)
            pipeline(pe, [(scatter_hot(p3b, FEAT, p3b.weighted), 0)])
            node_loop(n3b, 1, product_of(W2, FEAT))

        @block.vector
        def _(dve):
            steps = [0]

            def then(ins):
                steps[0] += 1
                ins.then_inc(s_step, 1)
                dve.wait_ge(s_step, steps[0])

            def load_tiles(row, i, q):
                _, v = nc.values_load_multi_w_load_instructions(
                    row[0:1, ds(8 * i + 2 * q, 2)], engines=[mybir.EngineType.DVE], min_val=0,
                    max_val=BUCKETS - 1, skip_runtime_bounds_check_because="the maps hold tiles")
                return v

            for s, v in presets:
                dve.sem_inc(s, v)

            dve.memset(region[:, 0:5 * COLS], 0.0).then_inc(s_step, 1)
            dve.memset(zeros, 0.0).then_inc(s_step, 1)
            dve.memset(ones, 1.0).then_inc(s_step, 1)
            dve.memset(sel, 0.0).then_inc(s_step, 1)
            dve.memset(padS, 0.0).then_inc(s_step, 1)
            dve.memset(blockdiag, 0.0).then_inc(s_step, 1)
            dve.memset(att, 0.0).then_inc(s_step, 1)
            steps[0] = 7
            dve.wait_ge(s_step, steps[0])
            then(dve.memset(G[:, :, :, FEAT:FEAT + 1], 1.0))
            then(dve.memset(region[:, 0:2 * COLS].bitcast(I32), PAD_NODE))
            padS_v = padS.rearrange("p (c k) -> p c k", k=SREC)
            padD_v = padD.rearrange("p (c k) -> p c k", k=DREC)
            for v in (padS_v, padD_v):
                then(dve.memset(v[:, :, 0].bitcast(I32), PAD_NODE))
                then(dve.memset(v[:, :, 1], -1.0))
            dve.sem_inc(s_setup, 1)
            dve.wait_ge(s_const, 3)
            then(dve.tensor_scalar(ident, diff, 0.0, None, ALU.is_equal))
            then(dve.tensor_scalar(upper, diff, 0.0, None, ALU.is_gt))
            then(dve.tensor_copy(iota16, iota))
            then(dve.tensor_copy(ident16, ident))
            dve.sem_inc(s_setup, 1)

            def place_edges(w, key, rec, pos):
                as_int = mask.bitcast(I32)
                cum_i = cum.bitcast(I32)
                then(dve.tensor_scalar(as_int, key, TILE_SHIFT, None, ALU.logical_shift_right))
                then(dve.tensor_copy(tile_f, as_int))
                then(dve.tensor_scalar(as_int, key, P - 1, None, ALU.bitwise_and))
                then(dve.tensor_copy(rec[:, :, 1], as_int))
                with dve.Fori(0, BUCKETS) as t:
                    dve.wait_ge(s_cnt, t + (w * BUCKETS + 1))
                    dve.tensor_scalar(mask, tile_f, iota[:, ds(t, 1)], 0.0, ALU.is_equal, ALU.add,
                                      accum_out=cnt[:, ds(t, 1)]).then_inc(s_cnt, 1)
                dve.wait_ge(s_cnt, (w + 1) * BUCKETS + 1)
                dve.sem_inc(s_prefix_in, 1)
                dve.wait_ge(s_prefix_out, w + 1)
                then(dve.tensor_scalar(size, banks[2][:, 0:BUCKETS], float(PAIR_EDGES - 1), None, ALU.add))
                then(dve.tensor_copy(size_i, size))
                then(dve.tensor_scalar(size_i, size_i, PAIR_SHIFT, None, ALU.logical_shift_right))
                then(dve.tensor_copy(size, size_i))
                then(dve.tensor_tensor_scan(ends, size, size, 0.0, ALU.add, ALU.max))
                then(dve.tensor_tensor(base, ends, size, ALU.subtract))
                then(dve.tensor_scalar(base, base, float(PAIR_EDGES), None, ALU.mult))
                then(dve.tensor_tensor(base, base, banks[3][:, 0:BUCKETS], ALU.add))
                shape = [P, MAPC, BUCKETS]
                then(dve.tensor_tensor(is_past, ends.unsqueeze(1).to_broadcast(shape),
                                       chunk_id.unsqueeze(2).to_broadcast(shape), ALU.is_le))
                then(dve.tensor_reduce(map_f, is_past, AX_X, ALU.add))
                then(dve.tensor_scalar(mapU[w], map_f, float(BUCKETS - 1), None, ALU.min))
                then(dve.memset(pos_f, 0.0))
                for b, (c0, c1) in enumerate(BLOCKS):
                    block = slice(c0, c1)
                    with dve.Fori(0, BUCKETS) as t:
                        k = t * 5 + (w * len(BLOCKS) + b) * 5 * BUCKETS
                        dve.tensor_scalar(mask[:, block], tile_f[:, block], iota[:, ds(t, 1)], None, ALU.is_equal
                                          ).then_inc(s_rank, 1)
                        dve.wait_ge(s_rank, k + 1)
                        dve.tensor_tensor_scan(cum[:, block], mask[:, block], mask[:, block], base[:, ds(t, 1)],
                                               ALU.add, ALU.max).then_inc(s_rank, 1)
                        dve.wait_ge(s_rank, k + 2)
                        dve.tensor_scalar(base[:, ds(t, 1)], cum[:, c1 - 1:c1], 0.0, None, ALU.add).then_inc(s_rank, 1)
                        dve.wait_ge(s_rank, k + 3)
                        dve.tensor_tensor(cum[:, block], cum[:, block], mask[:, block], ALU.mult).then_inc(s_rank, 1)
                        dve.wait_ge(s_rank, k + 4)
                        dve.tensor_tensor(pos_f[:, block], pos_f[:, block], cum[:, block], ALU.add).then_inc(s_rank, 1)
                        dve.wait_ge(s_rank, k + 5)
                    then(dve.tensor_scalar(pos_f[:, block], pos_f[:, block], -1.0, None, ALU.add))
                    then(dve.tensor_copy(pos[:, block], pos_f[:, block]))
                    then(dve.tensor_scalar(as_int[:, block], pos[:, block], P - 1, None, ALU.bitwise_and))
                    then(dve.tensor_scalar(cum_i[:, block], pos[:, block], TILE_SHIFT, None, ALU.logical_shift_right))
                    then(dve.scalar_tensor_tensor(out=pos[:, block], in0=as_int[:, block], scalar=float(CHUNKS),
                                                  in1=cum_i[:, block], op0=ALU.mult, op1=ALU.add))
                    if w == 0:
                        dve.sem_inc(s_nat[0], 1)

            dve.sem_inc(s_cnt, 1)
            dve.wait_ge(s_keys, 96)
            then(dve.tensor_copy(natD[:, :, 0].bitcast(I32), key_s))
            place_edges(0, key_d, natD, pos_d)
            then(dve.tensor_copy(natS[:, :, 0].bitcast(I32), key_d))
            place_edges(1, key_s, natS, pos_s)

            dve.wait_ge(s_kinds, 96)
            then(dve.tensor_copy(natS[:, :, 2:4], attr_in))
            then(dve.tensor_reduce(attr_sum, attr_in.rearrange("p c k -> p k c"), AX_X, ALU.add))
            dve.sem_inc(s_prefix_in, 1)
            dve.wait_ge(s_wload, 16 * WLOADS)
            then(dve.tensor_tensor(comps, comps, alpha.unsqueeze(2).to_broadcast([P, RELS, BASES]), ALU.mult))
            kind_f = cum
            then(dve.tensor_copy(kind_f, kind))
            then(dve.memset(natS[:, :, 4:8], 0.0))
            comps_flat = comps.rearrange("p r b -> p (r b)")
            with dve.Fori(0, RELS) as r:
                dve.tensor_scalar(mask, kind_f, iota[:, ds(r, 1)], None, ALU.is_equal).then_inc(s_coef, 1)
                dve.wait_ge(s_coef, r * 5 + 1)
                for b in range(BASES):
                    c = natS[:, :, 4 + b]
                    dve.scalar_tensor_tensor(out=c, in0=mask, scalar=comps_flat[:, ds(r * BASES + b, 1)], in1=c,
                                             op0=ALU.mult, op1=ALU.add).then_inc(s_coef, 1)
                dve.wait_ge(s_coef, r * 5 + 5)
            dve.sem_inc(s_nat[1], 1)

            for j in range(SCORES):
                h = j % HEADS
                part = slice(CH * h, CH * (h + 1))
                dve.tensor_copy(blockdiag[part, j:j + 1], attcol[part, (0 if j < HEADS else 1):(1 if j < HEADS else 2)]
                                ).then_inc(s_step, 1)
            steps[0] += SCORES
            dve.wait_ge(s_step, steps[0])
            dve.sem_inc(s_setup, 1)
            dve.wait_ge(s_prefix_out, 3)
            then(dve.tensor_scalar(attr_mean, banks[2][:, 0:2], 1.0 / E, None, ALU.mult))

            for q in range(RING):
                dve.wait_ge(s_nscat[0][q], 64 * NAT_ROUNDS[q])
            then(dve.tensor_copy(src_tile, tile_f))
            dve.wait_ge(s_fill, 16 * FILLS)
            then(dve.memset(acc_flat, 0.0))
            then(dve.memset(X[:, TILES - 1:BUCKETS, :], 0.0))
            dve.sem_inc(s_xpad, 1)
            dve.wait_ge(s_maps, 32)

            iota4 = iota.unsqueeze(1).to_broadcast([P, GROUP, P])

            def hot_of(ps, st, free):
                def f(i, q):
                    free(i, q)
                    dve.wait_ge(s_staged[q], ps.staged(i))
                    dve.tensor_tensor((hot16 if ps is p1a else hot)[:, q], iota4,
                                      st[:, q, :, 1:2].to_broadcast([P, GROUP, P]), ALU.is_equal
                                      ).then_inc(ps.hot, 1)
                return f

            def free_when_summed(ps):
                return lambda i, q: dve.wait_ge(ps.summed, when(i, q, 1))

            def free_when_turned(ps):
                return lambda i, q: dve.wait_ge(ps.turned, when(i, q, 1))

            def add_sums(ps, row, width):
                def f(i, q):
                    tiles = load_tiles(row, i, q)
                    dve.wait_ge(ps.summed, when(i, q, 5))
                    for j in range(PAIRS_OF_GROUP):
                        dve.wait_ge(ps.added, 8 * i + (2 * q + j + 8))
                        to = acc[:, ds(tiles[j], 1), 0:width]
                        dve.tensor_tensor(to, to, pair_out(q, j, width).unsqueeze(1), ALU.add).then_inc(ps.added, 1)
                return f

            iota4_16 = iota16.unsqueeze(1).to_broadcast([P, GROUP, P])

            def tile_and_place(i, q):
                dve.wait_ge(s_hist, when(i, q, 1))
                dve.tensor_tensor(place16[:, q], iota4_16,
                                  natS[:, ds(16 * i + 4 * q, 4), 1:2].to_broadcast([P, GROUP, P]), ALU.is_equal
                                  ).then_inc(s_hist_hot, 1)
                dve.tensor_tensor(tile16[:, q, :, 0:BUCKETS], iota4_16[:, :, 0:BUCKETS],
                                  src_tile[:, ds(16 * i + 4 * q, 4)].unsqueeze(2).to_broadcast([P, GROUP, BUCKETS]),
                                  ALU.is_equal).then_inc(s_hist_hot, 1)
            pipeline(dve, [(hot_of(p0, stD, free_when_summed(p0)), 3), (tile_and_place, 0, NAT_GROUPS),
                           (add_sums(p0, mapD, FEAT + 1), 0)])
            dve.wait_ge(p0.added, 2 * GROUPS + 8)
            dve.wait_ge(s_hist_out, 3)
            then(dve.tensor_copy(degs[:, :, 0], banks[6][:, 0:BUCKETS]))

            def over_rows(column, tiles=TILES, width=FEAT):
                return column[:, 0:tiles].unsqueeze(2).to_broadcast([P, tiles, width])

            def over_nodes(row, tiles=TILES):
                return row.unsqueeze(1).to_broadcast([P, tiles, FEAT])

            Xt = X[:, 0:TILES, :]
            acc_t = acc[:, 0:TILES, 0:FEAT]
            roots = [0]

            def take_root():
                roots[0] += 1
                dve.sem_inc(s_root_in, 1)
                dve.wait_ge(s_root_out, roots[0])

            def layer_norm():
                then(dve.tensor_reduce(col[:, 0:TILES], Xt, AX_X, ALU.add))
                then(dve.tensor_scalar(col[:, 0:TILES], col[:, 0:TILES], 1.0 / FEAT, None, ALU.mult))
                then(dve.tensor_tensor(Xt, Xt, over_rows(col), ALU.subtract))
                then(dve.tensor_tensor(ln_tmp, Xt, Xt, ALU.mult))
                then(dve.tensor_reduce(col[:, 0:TILES], ln_tmp, AX_X, ALU.add))
                then(dve.tensor_scalar(root[:, 0:TILES], col[:, 0:TILES], 1.0 / FEAT, EPS, ALU.mult, ALU.add))
                take_root()
                then(dve.reciprocal(col[:, 0:TILES], root[:, 0:TILES]))
                then(dve.tensor_tensor(Xt, Xt, over_rows(col), ALU.mult))

            def node_loop(nl, take):
                def f(t2, r):
                    dve.wait_ge(nl.product, t2 * 2 + (r + 3))
                    take(t2 * 2 + r, banks[2 + r])
                dve.sem_inc(nl.start, 1)
                pipeline(dve, [(f, 0)], groups=TILES, ring=2)
                dve.wait_ge(nl.taken, TILES + 2)

            def add_to(target, nl):
                def take(t, bank):
                    to = target[:, ds(t, 1), 0:FEAT]
                    dve.tensor_tensor(to, to, bank[:, 0:FEAT].unsqueeze(1), ALU.add).then_inc(nl.taken, 1)
                return take

            dve.wait_ge(s_x, 32)
            then(dve.tensor_copy(degs[:, :, 1], acc[:, :, FEAT]))
            then(dve.tensor_scalar(col, degs[:, :, 1], 1.0, None, ALU.max))
            then(dve.reciprocal(col2, col))
            then(dve.tensor_tensor(acc_t, acc_t, over_rows(col2), ALU.mult))
            node_loop(n0, add_to(X, n0))
            then(dve.tensor_tensor(Xt, Xt, over_nodes(rows["b0"]), ALU.add))
            layer_norm()

            then(dve.memset(acc_flat, 0.0))

            def take1(t, bank):
                dve.tensor_scalar(acc[:, ds(t, 1), 0:FEAT], bank[:, 0:FEAT].unsqueeze(1), 0.0, None, ALU.add)
                dve.tensor_scalar(att[:, ds(t, 1), :], bank[:, FEAT:FEAT + SCORES].unsqueeze(1), 0.0, None, ALU.add).then_inc(n1a.taken, 1)
            node_loop(n1a, take1)
            dve.sem_inc(s_tables, 1)

            def max_of_pair(j):
                def f(i, q):
                    if j == 0:
                        dve.wait_ge(p1a.hotT, when(i, q, 3))
                    dve.wait_ge(p1a.spread, 8 * i + (2 * q + j + 1))
                    dve.sem_inc(s_seen, 1)
                    for h in range(HEADS):
                        at_ = (h % 2) * PAIR_EDGES
                        ins = dve.tensor_tensor_reduce(
                            out=wide[:, h, 2 * j:2 * j + 2, :], in0=banks[2 * j + h // 2][:, at_:at_ + PAIR_EDGES]
                            .rearrange("p (u n) -> p u n", u=PAIR), in1=hotT[:, q % 2, PAIR * j:PAIR * (j + 1), :],
                            scale=1.0, scalar=-ABSENT, op0=ALU.add, op1=ALU.max,
                            accum_out=chunk_max[:, q % 2, j, h:h + 1])
                    ins.then_inc(p1a.weighted, 1)
                return f

            tiles_now = {}

            def raise_max(j):
                def f(i, q):
                    if j == 0:
                        tiles_now[0] = load_tiles(mapD, i, q)
                    dve.wait_ge(p1a.weighted, 8 * i + (2 * q + j + 5))
                    dve.wait_ge(s_max, 8 * i + (2 * q + j + 8))
                    to = att[:, ds(tiles_now[0][j], 1), HEADS:2 * HEADS]
                    dve.tensor_tensor(to, to, chunk_max[:, q % 2, j:j + 1, :], ALU.max).then_inc(s_max, 1)
                return f
            pipeline(dve, [(hot_of(p1a, stD, free_when_turned(p1a)), 4), (max_of_pair(0), 1), (raise_max(0), 0),
                           (max_of_pair(1), 1), (raise_max(1), 0)])
            dve.wait_ge(s_max, 2 * GROUPS + 8)

            a_dst, a_max, a_src = (att[:, :, k * HEADS:(k + 1) * HEADS] for k in range(3))
            then(dve.tensor_tensor(selfw, a_dst, a_max, ALU.add))
            then(dve.scalar_tensor_tensor(out=a_max, in0=selfw, scalar=0.2, in1=selfw, op0=ALU.mult, op1=ALU.max))
            then(dve.tensor_tensor(selfw, a_dst, a_src, ALU.add))
            then(dve.scalar_tensor_tensor(out=selfw2, in0=selfw, scalar=0.2, in1=selfw, op0=ALU.mult, op1=ALU.max))
            then(dve.tensor_tensor(selfw, selfw2, a_max, ALU.subtract))
            dve.sem_inc(s_self, 1)
            dve.wait_ge(s_selfexp, 1)
            for h in range(HEADS):
                then(dve.tensor_tensor(acc[:, 0:TILES, h * CH:(h + 1) * CH], acc[:, 0:TILES, h * CH:(h + 1) * CH],
                                       selfw2[:, 0:TILES, h:h + 1].to_broadcast([P, TILES, CH]), ALU.mult))
            then(dve.tensor_copy(acc[:, :, FEAT:ROW], selfw2))
            dve.sem_inc(s_selfexp, 1)

            def edge_args(i, q):
                dve.wait_ge(p1b.spread, when(i, q, 3))
                dve.wait_ge(s_exp, when(i, q, 1))
                dve.wait_ge(s_rows_loaded[q], 16 * i + 16)
                sc = banks[6 + q % 2][:, 0:GROUP * 2 * HEADS].rearrange("p (u k) -> p u k", u=GROUP)
                dve.tensor_tensor(e_sum[:, q % 2], G[:, q, :, FEAT:ROW],
                                  sc[:, :, 0:HEADS], ALU.add).then_inc(p1b.scaled, 1)
                dve.wait_ge(p1b.scaled, 8 * i + (2 * q + 1))
                dve.scalar_tensor_tensor(out=e_lrelu[:, q % 2], in0=e_sum[:, q % 2], scalar=0.2,
                                         in1=e_sum[:, q % 2], op0=ALU.mult, op1=ALU.max).then_inc(p1b.scaled, 1)
                dve.wait_ge(p1b.scaled, 8 * i + (2 * q + 2))
                dve.tensor_tensor(e_arg[:, q % 2], e_lrelu[:, q % 2], sc[:, :, HEADS:2 * HEADS], ALU.subtract
                                  ).then_inc(p1b.used, 1)

            def weight_rows(i, q):
                dve.wait_ge(s_exp, when(i, q, 3))
                r = G[:, q, :, 0:FEAT].rearrange("p u (h c) -> p u h c", h=HEADS)
                dve.tensor_tensor(r, r, G[:, q, :, FEAT:ROW].unsqueeze(3).to_broadcast([P, GROUP, HEADS, CH]),
                                  ALU.mult).then_inc(p1b.weighted, 1)
            pipeline(dve, [(weight_rows, 1), (hot_of(p1b, stD, free_when_summed(p1b)), 3),
                           (add_sums(p1b, mapD, ROW), 0), (edge_args, 2)])
            dve.wait_ge(p1b.added, 2 * GROUPS + 8)

            then(dve.tensor_scalar(selfw, acc[:, :, FEAT:ROW], 1e-16, None, ALU.add))
            then(dve.tensor_scalar(selfw[:, TILES:BUCKETS, :], selfw[:, TILES:BUCKETS, :], 1.0, None, ALU.max))
            then(dve.reciprocal(selfw2, selfw))
            for h in range(HEADS):
                then(dve.tensor_tensor(acc[:, 0:TILES, h * CH:(h + 1) * CH], acc[:, 0:TILES, h * CH:(h + 1) * CH],
                                       selfw2[:, 0:TILES, h:h + 1].to_broadcast([P, TILES, CH]), ALU.mult))
            node_loop(n1b, add_to(acc, n1b))
            then(dve.tensor_tensor(acc_t, acc_t, over_nodes(rows["bias1"]), ALU.add))
            dve.sem_inc(s_bn_in, 1)
            dve.wait_ge(s_bn_out, 1)
            then(dve.tensor_scalar(mean_row, banks[4][:, 0:FEAT], 1.0 / N, None, ALU.mult))
            then(dve.tensor_tensor(acc_t, acc_t, over_nodes(mean_row), ALU.subtract))
            then(dve.tensor_tensor(squares, acc_t, acc_t, ALU.mult))
            dve.sem_inc(s_bn_in, 1)
            dve.wait_ge(s_bn_out, 2)
            then(dve.tensor_scalar(root, banks[4][:, 0:FEAT], 1.0 / N, EPS, ALU.mult, ALU.add))
            take_root()
            then(dve.reciprocal(scale_row, root))
            then(dve.tensor_tensor(scale_row, scale_row, rows["gamma1"], ALU.mult))
            then(dve.tensor_tensor(acc_t, acc_t, over_nodes(scale_row), ALU.mult))
            then(dve.tensor_tensor(acc_t, acc_t, over_nodes(rows["beta1"]), ALU.add))
            then(dve.tensor_tensor(Xt, Xt, acc_t, ALU.add))
            layer_norm()

            then(dve.tensor_scalar(root[:, 0:BUCKETS], degs[:, :, 0], 1.0, None, ALU.max))
            take_root()
            then(dve.reciprocal(col, root[:, 0:BUCKETS]))
            then(dve.tensor_scalar(col2, degs[:, :, 0], 0.0, None, ALU.is_gt))
            then(dve.tensor_tensor(dinv, col, col2, ALU.mult))
            then(dve.tensor_tensor(ln_tmp, Xt, over_rows(dinv), ALU.mult))
            dve.sem_inc(s_tables, 1)
            dve.wait_ge(s_stored, 48)
            for q in range(RING):
                dve.wait_ge(s_nscat[1][q], 64 * NAT_ROUNDS[q])
            then(dve.memset(rel_flat, 0.0))

            def add_relations(i, q):
                tiles = load_tiles(mapS, i, q)
                for j in range(PAIRS_OF_GROUP):
                    dve.wait_ge(p2.used, 16 * i + (4 * q + 2 * j + 10))
                    dve.wait_ge(p2.added, 8 * i + (2 * q + j + 8))
                    to = rel_acc[:, ds(tiles[j], 1), :]
                    dve.tensor_tensor(to, to, banks[2 * (q % 2) + j].unsqueeze(1), ALU.add).then_inc(p2.added, 1)
            def scale_last(i, q):
                dve.wait_ge(p2.hot, when(i, q, 1))
                dve.wait_ge(p2.used, 16 * i + (4 * q + 4))
                dve.tensor_tensor(sq[:, q % 2], hot[:, q], stS[:, q, :, SREC - 1:SREC].to_broadcast([P, GROUP, P]),
                                  ALU.mult).then_inc(s_last_base, 1)

            def free_when_scaled(i, q):
                dve.wait_ge(p2.scaled, 16 * i + (4 * q + 4))
                dve.wait_ge(s_last_base, when(i, q, 1))
            pipeline(dve, [(scale_last, 1), (hot_of(p2, stS, free_when_scaled), 2), (add_relations, 0)])
            dve.wait_ge(p2.added, 2 * GROUPS + 8)

            def take2(t, bank):
                to = X[:, ds(t, 1), :]
                dve.scalar_tensor_tensor(out=to, in0=bank[:, 0:FEAT].unsqueeze(1), scalar=dinv[:, ds(t, 1)],
                                         in1=to, op0=ALU.mult, op1=ALU.add).then_inc(n2.taken, 1)
            node_loop(n2, take2)
            layer_norm()

            def take3(t, bank):
                dve.tensor_scalar(Pt[:, ds(t, 1), :], bank[:, 0:FEAT].unsqueeze(1), 0.0, None, ALU.add)
                dve.tensor_scalar(acc[:, ds(t, 1), 0:FEAT], bank[:, FEAT:2 * FEAT].unsqueeze(1), 0.0, None, ALU.add).then_inc(n3a.taken, 1)
            node_loop(n3a, take3)
            dve.sem_inc(s_tables, 1)
            then(dve.tensor_tensor(weighted_pq, Pt[:, 0:TILES, :],
                                   degs[:, 0:TILES, 0:1].to_broadcast([P, TILES, FEAT]), ALU.mult))
            then(dve.tensor_tensor(weighted_q, acc_t, degs[:, 0:TILES, 1:2].to_broadcast([P, TILES, FEAT]), ALU.mult))
            then(dve.tensor_tensor(weighted_pq, weighted_pq, weighted_q, ALU.add))
            dve.sem_inc(s_mu_in, 1)
            dve.wait_ge(s_mu, 1)
            then(dve.tensor_scalar(mean_row, banks[4][:, 0:FEAT], 1.0 / E, None, ALU.mult))
            for k, n in enumerate(("w_attr0", "w_attr1")):
                then(dve.scalar_tensor_tensor(out=mean_row, in0=rows[n], scalar=attr_mean[:, k:k + 1],
                                              in1=mean_row, op0=ALU.mult, op1=ALU.add))
            then(dve.tensor_tensor(mean_row, mean_row, rows["b1"], ALU.add))
            then(dve.tensor_tensor(mean_row, rows["b1"], mean_row, ALU.subtract))
            then(dve.tensor_tensor(Pt[:, 0:TILES, :], Pt[:, 0:TILES, :], over_nodes(mean_row), ALU.add))
            then(dve.memset(Pt[:, TILES:BUCKETS, :], 0.0))
            dve.sem_inc(s_mu_in, 1)

            def make_hidden(i, q):
                dve.wait_ge(p3a.summed, when(i, q, 5))
                dve.wait_ge(s_gathered[q], p3a.gathered(i))
                dve.wait_ge(s_hstored[q], 16 * i + 16)
                dve.wait_ge(s_square, when(i, q, 1))
                dve.tensor_tensor(wide[:, q], banks[q % 2].rearrange("p (u n) -> p u n", u=GROUP),
                                  G[:, q, :, 0:FEAT], ALU.add).then_inc(p3a.added, PAIRS_OF_GROUP)
            pipeline(dve, [(hot_of(p3a, stS, free_when_turned(p3a)), 3), (make_hidden, 0)])

            dve.wait_ge(s_mu, 2)
            then(dve.tensor_reduce(mean_row, banks[3].rearrange("p (u f) -> p f u", u=GROUP), AX_X, ALU.add))
            then(dve.tensor_scalar(root, mean_row, 1.0 / E, EPS, ALU.mult, ALU.add))
            take_root()
            then(dve.reciprocal(scale_row, root))
            then(dve.tensor_tensor(scale_row, scale_row, rows["gamma3"], ALU.mult))
            then(dve.memset(acc_flat, 0.0))

            dve.sem_inc(s_scale_row, 1)

            def shift_hidden(i, q):
                dve.wait_ge(p3b.used, when(i, q, 1))
                dve.tensor_tensor(wide[:, q], wide[:, q], over_nodes(rows["beta3"], GROUP), ALU.add
                                  ).then_inc(p3b.scaled, 1)
            pipeline(dve, [(hot_of(p3b, stS, free_when_summed(p3b)), 3), (shift_hidden, 2),
                           (add_sums(p3b, mapS, FEAT), 0)])
            dve.wait_ge(p3b.added, 2 * GROUPS + 8)
            then(dve.tensor_scalar(col, degs[:, :, 0], 1.0, None, ALU.add))
            then(dve.reciprocal(col2, col))

            def take4(t, bank):
                k = 2 * t
                dve.scalar_tensor_tensor(out=mean_row, in0=rows["b2"], scalar=degs[:, ds(t, 1), 0],
                                         in1=bank[:, 0:FEAT], op0=ALU.mult, op1=ALU.add).then_inc(s_last, 1)
                dve.wait_ge(s_last, k + 1)
                to = X[:, ds(t, 1), :]
                dve.scalar_tensor_tensor(out=scale_row.unsqueeze(1), in0=mean_row.unsqueeze(1),
                                         scalar=col2[:, ds(t, 1)], in1=to, op0=ALU.mult, op1=ALU.add
                                         ).then_inc(s_last, 1)
                dve.wait_ge(s_last, k + 2)
                dve.tensor_tensor(to, to, scale_row.unsqueeze(1), ALU.add).then_inc(n3b.taken, 1)
                dve.wait_ge(n3b.taken, t + 3)
            node_loop(n3b, take4)
            layer_norm()
            dve.sem_inc(s_final, 1)


_INS = ["x", "src", "dst", "edge_attr_2", "edge_type_50", "L0_gnn_W", "L0_gnn_b", "L1_gnn_W_src",
        "L1_gnn_att_src", "L1_gnn_att_dst", "L1_gnn_W_res", "L1_gnn_bias", "L1_gnn_gamma", "L1_gnn_beta",
        "L2_gnn_bases", "L2_gnn_comps", "L2_gnn_alpha", "L3_gnn_W1", "L3_gnn_b1", "L3_gnn_gamma",
        "L3_gnn_beta", "L3_gnn_W2", "L3_gnn_b2"]


def kernel(**inputs):
    import numpy as _np
    import concourse.bacc as _bacc
    from concourse import mybir as _mybir
    from concourse.bass_utils import run_bass_kernel_spmd as _run

    nc = _bacc.Bacc("TRN2", target_bir_lowering=False, num_devices=1)
    arrays, args = {}, []
    for name in _INS:
        a = _np.ascontiguousarray(inputs[name])
        arrays[f"in_{name}_dram"] = a
        args.append(nc.dram_tensor(f"in_{name}_dram", a.shape, _mybir.dt.from_np(a.dtype), kind="ExternalInput").ap())
    out = nc.dram_tensor("out_0_dram", inputs["x"].shape, _mybir.dt.float32, kind="ExternalOutput").ap()
    gnn_program(nc, *args, out)
    r = _run(nc, [arrays], core_ids=[0])
    return r.results[0]["out_0_dram"]
```
